# Optimizing a Trainium2 kernel written in Bass

```python
import numpy as np
import jax
import jax.numpy as jnp

def _softmax(x, axis=-1):
    return jax.nn.softmax(x, axis=axis)

def _gelu(x):
    return jax.nn.gelu(x, approximate=True)

def _silu(x):
    return jax.nn.silu(x)

def _sigmoid(x):
    return jax.nn.sigmoid(x)

def _layernorm(x, axis=-1, eps=1e-05):
    m = jnp.mean(x, axis=axis, keepdims=True)
    v = jnp.var(x, axis=axis, keepdims=True)
    return (x - m) / jnp.sqrt(v + eps)

def _scatter_add(tgt, idx, src, axis=0):
    return tgt.at[idx].add(src)

def _segment_sum(src, seg, n):
    return jax.ops.segment_sum(src, seg, n)
kernel_name = 'mk_adj_resnorm_d4_adj_r2_e26872'

def setup_inputs(seed: int=0):
    np.random.seed(seed)
    _w = jnp.asarray

    def _rec_inputs():
        import jax
        import jax.numpy as jnp
        _gk = jax.random.key(seed)
        x = 7.22e-05 + 1 * jax.random.normal(jax.random.fold_in(_gk, 1), (32, 256, 256), jnp.float32)
        _a = jax.random.bernoulli(jax.random.fold_in(_gk, 2), 0.015625, (32, 256, 256))
        _a = jnp.logical_or(_a, jnp.swapaxes(_a, -1, -2))
        _a = jnp.logical_or(_a, jnp.eye(256, dtype=bool))
        _af = _a.astype(jnp.float32)
        _af = _af * jax.random.uniform(jax.random.fold_in(_gk, 3), (32, 256, 256), jnp.float32, 0.05, 1)
        adj = _af
        return (x, adj)
    x, adj = _rec_inputs()

    def _L0_gnn_setup():
        import jax, jax.numpy as jnp
        import numpy as np
        B, N, D_IN, D_OUT = (4, 2048, 256, 256)
        key = jax.random.key(seed)
        k1, k2, k3, k4 = jax.random.split(key, 4)
        x = jax.random.normal(k1, (B, N, D_IN), dtype=jnp.float32)
        A_shape = jax.random.uniform(k2, (B, N, N), dtype=jnp.float32)
        w = jax.random.normal(k3, (D_IN, D_OUT), dtype=jnp.float32)
        a = jax.random.normal(k4, (D_OUT,), dtype=jnp.float32)
        return {'x': x, 'A_shape': A_shape, 'w': w, 'a': a}
    _L0_gnn_all = _L0_gnn_setup()
    _L0_gnn_in = {k: v for k, v in _L0_gnn_all.items() if k in ('w', 'a')}
    del _L0_gnn_all

    def _L1_gnn_setup():
        import jax, jax.numpy as jnp
        import numpy as np
        B, N, F_IN, F_HID, F_OUT = (32, 512, 256, 256, 256)

        def _gcn_layer(x, adj, W, b):
            support = jnp.einsum('bnf,fh->bnh', x, W)
            return jnp.einsum('bnm,bmh->bnh', adj, support) + b
        key = jax.random.key(seed)
        ks = jax.random.split(key, 8)

        def xavier(k, fan_in, fan_out):
            bound = float(np.sqrt(6.0 / (fan_in + fan_out)))
            return jax.random.uniform(k, (fan_in, fan_out), jnp.float32, -bound, bound)
        return {'batch_graph': jax.random.normal(ks[0], (B, N, F_IN), jnp.float32), 'adj': jax.random.uniform(ks[1], (B, N, N), jnp.float32), 'W1': xavier(ks[2], F_IN, F_HID), 'b1': jnp.zeros((F_HID,), jnp.float32), 'W2': xavier(ks[3], F_HID, F_HID), 'b2': jnp.zeros((F_HID,), jnp.float32), 'W3': xavier(ks[4], F_HID, F_OUT), 'b3': jnp.zeros((F_OUT,), jnp.float32)}
    _L1_gnn_all = _L1_gnn_setup()
    _L1_gnn_in = {k: v for k, v in _L1_gnn_all.items() if k in ('W1', 'b1', 'W2', 'b2', 'W3', 'b3')}
    del _L1_gnn_all

    def _L2_gnn_setup():
        import jax, jax.numpy as jnp
        import numpy as np
        B, N, DIN, DOUT = (8, 1024, 256, 256)
        EDGE_P = 0.01

        def _gcn_norm(adj):
            A = (adj != 0).astype(adj.dtype)
            eye = jnp.eye(A.shape[-1], dtype=A.dtype)
            A = jnp.maximum(A, eye)
            deg = A.sum(axis=-1)
            dinv = jnp.where(deg > 0, jax.lax.rsqrt(deg), 0.0)
            return dinv[..., :, None] * A * dinv[..., None, :]
        key = jax.random.key(seed)
        k1, k2, k3, k4 = jax.random.split(key, 4)
        inputs = jax.random.normal(k1, (B, N, DIN), dtype=jnp.float32)
        adj = (jax.random.uniform(k2, (B, N, N)) < EDGE_P).astype(jnp.float32)
        W = jax.random.normal(k3, (DIN, DOUT), dtype=jnp.float32) / np.sqrt(DIN)
        b = jax.random.normal(k4, (DOUT,), dtype=jnp.float32) * 0.01
        return {'inputs': inputs, 'adj': adj, 'W': W, 'b': b}
    _L2_gnn_all = _L2_gnn_setup()
    _L2_gnn_in = {k: v for k, v in _L2_gnn_all.items() if k in ('W', 'b')}
    del _L2_gnn_all

    def _L3_gnn_setup():
        import jax, jax.numpy as jnp
        import numpy as np
        EPS = 1e-06
        key = jax.random.key(seed)
        k1, k2, k3 = jax.random.split(key, 3)
        B, N, F, O = (8, 2048, 256, 256)
        x = jax.random.normal(k1, (B, N, F), dtype=jnp.float32)
        adj = jax.random.uniform(k2, (B, N, N), dtype=jnp.float32)
        W = jax.random.normal(k3, (O, 2 * F), dtype=jnp.float32) * (1.0 / np.sqrt(2 * F))
        return {'x': x, 'adj': adj, 'W': W}
    _L3_gnn_all = _L3_gnn_setup()
    _L3_gnn_in = {k: v for k, v in _L3_gnn_all.items() if k in ('W',)}
    del _L3_gnn_all
    return {'x': x, 'adj': adj, 'L0_gnn_w': _L0_gnn_in['w'], 'L0_gnn_a': _L0_gnn_in['a'], 'L1_gnn_W1': _L1_gnn_in['W1'], 'L1_gnn_b1': _L1_gnn_in['b1'], 'L1_gnn_W2': _L1_gnn_in['W2'], 'L1_gnn_b2': _L1_gnn_in['b2'], 'L1_gnn_W3': _L1_gnn_in['W3'], 'L1_gnn_b3': _L1_gnn_in['b3'], 'L2_gnn_W': _L2_gnn_in['W'], 'L2_gnn_b': _L2_gnn_in['b'], 'L3_gnn_W': _L3_gnn_in['W']}

def reference(x, adj, L0_gnn_w, L0_gnn_a, L1_gnn_W1, L1_gnn_b1, L1_gnn_W2, L1_gnn_b2, L1_gnn_W3, L1_gnn_b3, L2_gnn_W, L2_gnn_b, L3_gnn_W):
    import jax
    import jax.numpy as jnp

    def _L0_gnn_ref(x, A_shape, w, a):
        import jax, jax.numpy as jnp
        import numpy as np
        B, N, D_IN, D_OUT = (4, 2048, 256, 256)
        y = x @ w
        s = y @ a
        A = s[..., :, None] + s[..., None, :]
        A = jnp.tanh(A / 8.0) * 8.0
        A = jnp.where(A >= 0, A, 0.1 * A)
        A = jnp.exp(A) * A_shape
        A = A / jnp.sum(A, axis=-1, keepdims=True)
        A = A * jnp.sum(A_shape, axis=-1, keepdims=True)
        out = A @ x @ w
        return out

    def _L1_gnn_ref(batch_graph, adj, W1, b1, W2, b2, W3, b3):
        import jax, jax.numpy as jnp
        import numpy as np
        B, N, F_IN, F_HID, F_OUT = (32, 512, 256, 256, 256)

        def _gcn_layer(x, adj, W, b):
            support = jnp.einsum('bnf,fh->bnh', x, W)
            return jnp.einsum('bnm,bmh->bnh', adj, support) + b
        x = jax.nn.relu(_gcn_layer(batch_graph, adj, W1, b1))
        x = jax.nn.relu(_gcn_layer(x, adj, W2, b2))
        out = _gcn_layer(x, adj, W3, b3)
        return out

    def _L2_gnn_ref(inputs, adj, W, b):
        import jax, jax.numpy as jnp
        import numpy as np
        B, N, DIN, DOUT = (8, 1024, 256, 256)
        EDGE_P = 0.01

        def _gcn_norm(adj):
            A = (adj != 0).astype(adj.dtype)
            eye = jnp.eye(A.shape[-1], dtype=A.dtype)
            A = jnp.maximum(A, eye)
            deg = A.sum(axis=-1)
            dinv = jnp.where(deg > 0, jax.lax.rsqrt(deg), 0.0)
            return dinv[..., :, None] * A * dinv[..., None, :]
        norm = _gcn_norm(adj)
        h = jnp.einsum('bnf,fo->bno', inputs, W)
        agg = jnp.einsum('bnm,bmo->bno', norm, h)
        return jnp.tanh(agg + b)

    def _L3_gnn_ref(x, adj, W):
        import jax, jax.numpy as jnp
        import numpy as np
        EPS = 1e-06
        deg = jnp.sum(adj, axis=-1, keepdims=True)
        agg = jnp.einsum('bij,bjf->bif', adj, x) / jnp.maximum(deg, EPS)
        cat = jnp.concatenate([x, agg], axis=2)
        out = jnp.einsum('bnf,of->bno', cat, W)
        return jax.nn.relu(out)
    x = _layernorm(x + _L0_gnn_ref(x, adj, L0_gnn_w, L0_gnn_a), axis=-1)
    x = _layernorm(x + _L1_gnn_ref(x, adj, L1_gnn_W1, L1_gnn_b1, L1_gnn_W2, L1_gnn_b2, L1_gnn_W3, L1_gnn_b3), axis=-1)
    x = _layernorm(x + _L2_gnn_ref(x, adj, L2_gnn_W, L2_gnn_b), axis=-1)
    x = _layernorm(x + _L3_gnn_ref(x, adj, L3_gnn_W), axis=-1)
    return x

_drawn_inputs = setup_inputs


def setup_inputs(seed=0):
    import zlib

    import numpy as np

    out = dict(_drawn_inputs(seed))
    spreads = {'L1_gnn_b1': (0.0, 0.1), 'L1_gnn_b2': (0.0, 0.48), 'L1_gnn_b3': (0.0, 0.8)}
    factors = {'L2_gnn_b': 8.0}
    for name, (base, spread) in spreads.items():
        noise = np.random.default_rng([zlib.crc32(name.encode()), seed]).standard_normal(out[name].shape)
        drawn = base * np.exp(spread * noise) if base else spread * noise
        out[name] = jnp.asarray(drawn.astype(out[name].dtype))
    for name, factor in factors.items():
        out[name] = (out[name] * factor).astype(out[name].dtype)
    return out
```

```python
from contextlib import ExitStack

import concourse.bass as bass
from concourse import mybir

P = 128
F32 = mybir.dt.float32
F32R = mybir.dt.float32r
ALU = mybir.AluOpType
ACT = mybir.ActivationFunctionType

LN_EPS = 1e-5
DEG_EPS = 1e-6
RING = 4


def exists(g):
    return not isinstance(g, int) or g >= 0


def resnorm_gnn_stack(nc, x, adj, w0, a0, w1, b1, w2, b2, w3, b3, wg, bg, wc, out):
    G, N, F = x.shape
    NT = N // P
    assert NT == 2 and F == N
    QUADS = G // RING

    with ExitStack() as ctx:
        def sb(name, shape, dt=F32):
            return ctx.enter_context(nc.sbuf_tensor(name, [P, *shape], dt))

        def split(name, width=F):
            return sb(name + "_hi", [NT, width], F32R), sb(name + "_lo", [NT, width], F32R)

        def sem(name):
            return ctx.enter_context(nc.semaphore(name))

        eye = sb("eye", [NT, N])
        ident = eye[:, 0, 0:P]
        ones = sb("ones", [2])
        ones_r = sb("ones_r", [2], F32R)
        zero2 = sb("zero2", [NT])
        eps2 = sb("eps2", [NT])
        minus_half2 = sb("minus_half2", [NT])
        wait_pad = sb("wait_pad", [1])
        w0_raw = sb("w0_raw", [NT, F + 2])
        wa_col = sb("wa_col", [NT])
        raws = {n: sb(n + "_raw", [NT, F]) for n in ("w1", "w2", "w3", "wg")}
        wc_raw = sb("wc_raw", [NT, 2 * F])
        junk = sb("junk", [F])
        a_rows = sb("a_rows", [F])
        b3_rows = sb("b3_rows", [NT, F])
        bg_rows = sb("bg_rows", [NT, F])
        b1_col = sb("b1_col", [NT])
        b2_col = sb("b2_col", [NT])
        W0 = split("w0", F + 2)
        W1, W2, W3, WG = split("w1"), split("w2"), split("w3"), split("wg")
        WS, WN = split("w_self"), split("w_neigh")

        x_in = [sb(f"x_in{k}", [NT, F]) for k in range(RING)]
        adj_in = [sb(f"adj_in{k}", [NT, N]) for k in range(RING)]
        adjT = [split(f"adjT{k}", N) for k in range(RING)]
        linkT = [sb(f"linkT{k}", [NT, N], F32R) for k in range(RING)]
        rowsum = [sb(f"rowsum{k}", [NT]) for k in range(RING)]
        inv_deg = [sb(f"inv_deg{k}", [NT]) for k in range(RING)]
        adjT_full = [sb(f"adjT_full{k}", [NT, N]) for k in range(2)]
        xT, x1T, x2T, x3T = split("xT"), split("x1T"), split("x2T"), split("x3T")
        y = sb("y_hi", [NT, F + 2], F32R), sb("y_lo", [NT, F], F32R)
        s_col = sb("s_col", [NT])
        gate = sb("gate", [NT, N])
        gate_leaky = sb("gate_leaky", [NT, N])
        unused = sb("unused", [NT, N])
        eT_full = sb("eT_full", [NT, N])
        eT = split("eT", N)
        inv_esum = sb("inv_esum", [NT])
        ratio = sb("ratio", [NT])
        sup1, sup2, sup3 = split("sup1"), split("sup2"), split("sup3")
        h1T_full, h2T_full = sb("h1T_full", [NT, N]), sb("h2T_full", [NT, N])
        h1T, h2T = split("h1T", N), split("h2T", N)
        deg = sb("deg", [NT])
        dinv = [sb(f"dinv{k}", [NT]) for k in range(2)]
        msg = split("msg")
        agg = sb("agg", [NT, F])
        z = split("z")
        u_self = sb("u_self", [NT, F])
        pre_relu = sb("pre_relu", [NT, F])
        deg_floor = sb("deg_floor", [NT])
        res = [sb(f"res{n}", [NT, F]) for n in range(4)]
        x1 = sb("x1", [NT, F])
        x1_b3 = [sb(f"x1_b3_{k}", [NT, F]) for k in range(2)]
        x2 = [sb(f"x2_{k}", [NT, F]) for k in range(2)]
        x3 = [sb(f"x3_{k}", [NT, F]) for k in range(2)]
        x4 = [sb(f"x4_{k}", [NT, F]) for k in range(2)]
        stats = [sb(f"stats{n}", [NT, 6]) for n in range(4)]
        mean_var = [sb(f"mean_var{n}", [NT, 2]) for n in range(4)]
        var_eps = [sb(f"var_eps{n}", [NT]) for n in range(4)]
        neg_mean = [sb(f"neg_mean{n}", [NT]) for n in range(4)]
        rstd = [sb(f"rstd{n}", [NT]) for n in range(4)]
        shift = [sb(f"shift{n}", [NT]) for n in range(4)]

        BANK = 512
        psX = ctx.enter_context(nc.psum_tensor("psX", [P, 2, BANK], F32))
        psB = ctx.enter_context(nc.psum_tensor("psB", [P, 2, BANK], F32))
        psA, psC, psD, psU = (ctx.enter_context(nc.psum_tensor(n, [P, NT, F], F32)) for n in ("psA", "psC", "psD", "psU"))
        s_bcast = psX[:, 0, 0:N]

        in_sem = [sem(f"loaded{k}") for k in range(RING)]
        out_sem = [sem(f"stored{k}") for k in range(2)]
        w_sem, consts_sem, setup_w_sem, setup_hi_sem, setup_lo_sem, setup_pe_sem, wa_sem = (
            sem(n) for n in ("weights_loaded", "consts_ready", "w0_widened", "weights_hi", "weights_lo",
                             "wc_turned", "wa_ready"))
        eye_sem = sem("eye_cleared")
        (xT_mm, adjT_mm, y_mm, s_mm, Ay_mm, x1T_mm, sup1_mm, h1_mm, sup2_mm, h2_mm, sup3_mm, o3_mm, deg_mm,
         x2T_mm, msg_mm, agg_mm, x3T_mm, z_mm, u_mm, v_mm) = (sem(n) for n in (
            "xT_mm", "adjT_mm", "y_mm", "s_mm", "Ay_mm", "x1T_mm", "sup1_mm", "h1_mm", "sup2_mm", "h2_mm",
            "sup3_mm", "o3_mm", "deg_mm", "x2T_mm", "msg_mm", "agg_mm", "x3T_mm", "z_mm", "u_mm", "v_mm"))
        (xT_hi, adjT_ok, rowsum_ok, y_hi, gate_tanh, gate_ok, x1_ok, x1T_hi, sup1_hi, h1_full,
         sup2_hi, h2_full, sup3_hi, x2_ok, x2T_hi, msg_hi, agg_tanh, x3_ok, x3T_hi, z_hi, u_ok, x4_ok) = (
            sem(n) for n in ("xT_hi", "adjT_ok", "rowsum_ok", "y_hi", "gate_tanh", "gate_ok",
                             "x1_ok", "x1T_hi", "sup1_hi", "h1_full", "sup2_hi", "h2_full", "sup3_hi", "x2_ok",
                             "x2T_hi", "msg_hi", "agg_tanh", "x3_ok", "x3T_hi", "z_hi", "u_ok", "x4_ok"))
        (xT_lo, link_ok, adj_hi, gate_leaky_ok, s_ok, e_full, e_hi, esum_ok, ratio_ok, x1T_lo, sup1_lo, h1_hi, sup2_lo,
         h2_hi, sup3_lo, deg_ok, x2T_lo, msg_lo, agg_scaled, x3T_lo, z_lo, floor_ok, inv_deg_ok, v_ok) = (
            sem(n) for n in ("xT_lo", "link_ok", "adj_hi", "gate_leaky_ok", "s_ok", "e_full", "e_hi", "esum_ok", "ratio_ok",
                             "x1T_lo", "sup1_lo", "h1_hi", "sup2_lo", "h2_hi", "sup3_lo", "deg_ok", "x2T_lo",
                             "msg_lo", "agg_scaled", "x3T_lo", "z_lo", "floor_ok", "inv_deg_ok", "v_ok"))
        res_ok = [sem(f"res_ok{n}") for n in range(4)]
        stats_ok = [sem(f"stats_ok{n}") for n in range(4)]
        mv_ok = [sem(f"mean_var_ok{n}") for n in range(4)]
        adj_lo, e_lo, h1_lo, h2_lo, x1_b3_ok, dinv_ok = (
            sem(n) for n in ("adj_lo", "e_lo", "h1_lo", "h2_lo", "x1_b3_ok", "dinv_ok"))
        var_ok = [sem(f"var_ok{n}") for n in range(4)]
        rstd_ok = [sem(f"rstd_ok{n}") for n in range(4)]
        shift_ok = [sem(f"shift_ok{n}") for n in range(4)]

        N_WLOADS = 12
        N_CONSTS = 8
        block = ctx.enter_context(nc.Block())

        def steps(eng, step):
            for k in range(RING):
                step(k, 0, k)
            with eng.Fori(1, QUADS) as q:
                for k in range(RING):
                    step(q * RING + k, q, k)
            for k in range(RING):
                step(G + k, QUADS, k)

        def live(g):
            return not isinstance(g, int) or 0 <= g < G

        @block.sync
        def _(sp):
            def load(q, k):
                sp.dma_start(x_in[k][:], x_q[q, k]).then_inc(in_sem[k], 16)
                sp.dma_start(adj_in[k][:], adj_q[q, k]).then_inc(in_sem[k], 16)

            x_q = x.rearrange("(q k) (t p) f -> q k p t f", k=RING, p=P)
            adj_q = adj.rearrange("(q k) (t p) f -> q k p t f", k=RING, p=P)

            def rows(v):
                return v.rearrange("(a f) -> a f", a=1).broadcast_to([P, F])

            def cols(v):
                return v.rearrange("(t p) -> p t", p=P)

            load(0, 0)
            sp.dma_start(w0_raw[:, :, 0:F], w0.rearrange("(t p) h -> p t h", p=P)).then_inc(w_sem, 16)
            sp.dma_start(a_rows[:], rows(a0)).then_inc(w_sem, 16)
            for n, w in (("w1", w1), ("w2", w2), ("w3", w3), ("wg", wg)):
                sp.dma_start(raws[n][:], w.rearrange("(t p) h -> p t h", p=P)).then_inc(w_sem, 16)
            sp.dma_start(wc_raw[:], wc.rearrange("(t p) f -> p t f", p=P)).then_inc(w_sem, 16)
            with nc.allow_non_contiguous_dma(reason="two short columns, once"):
                sp.dma_start(b1_col[:], cols(b1)).then_inc(w_sem, 16)
                sp.dma_start(b2_col[:], cols(b2)).then_inc(w_sem, 16)
            sp.dma_start(b3_rows[:, 0, :], rows(b3)).then_inc(w_sem, 16)
            sp.dma_start(b3_rows[:, 1, :], rows(b3)).then_inc(w_sem, 16)
            sp.dma_start(bg_rows[:, 0, :], rows(bg)).then_inc(w_sem, 16)
            sp.dma_start(bg_rows[:, 1, :], rows(bg)).then_inc(w_sem, 16)
            for k in range(1, RING):
                load(0, k)
            with sp.Fori(1, QUADS) as q:
                for k in range(RING):
                    g = q * RING + k - RING
                    sp.wait_ge(adjT_mm, g + 1)
                    sp.wait_ge(rowsum_ok, g + 1)
                    sp.wait_ge(res_ok[0], g + 1)
                    load(q, k)

        @block.tensor
        def _(pe):
            def turn(dst, src, done):
                for rt in range(NT):
                    for ct in range(NT):
                        mm = pe.transpose(dst[:, ct, rt * P:(rt + 1) * P], src[:, rt, ct * P:(ct + 1) * P], ident)
                mm.then_inc(done, 1)

            def product(dst, left, right, done, widths=(F, F)):
                passes = [(l, r) for l in range(len(left)) for r in range(len(right)) if l + r < 2]
                for rt in range(NT):
                    n = 0
                    for ct in range(NT):
                        for l, r in passes:
                            w = widths[r]
                            mm = pe.matmul(dst[:, rt, 0:w], left[l][:, ct, rt * P:(rt + 1) * P],
                                           right[r][:, ct, 0:w], start=(n == 0), stop=(n == NT * len(passes) - 1),
                                           skip_group_check=True)
                            n += 1
                mm.then_inc(done, 1)

            def step(t, q, k):
                if live(t):
                    g, slot = t, k
                    pe.wait_ge(in_sem[slot], 32 * q + 32)
                    if exists(g - 1):
                        pe.wait_ge(gate_tanh, g)
                    turn(psX[:, 0, :].rearrange("p (t n) -> p t n", t=NT), x_in[slot], xT_mm)
                    if exists(g - 4):
                        pe.wait_ge(x2T_lo, g - 3)
                    turn(psA, adj_in[slot], adjT_mm)
                if live(t - 4):
                    g = t - 4
                    if live(g + 1):
                        pe.wait_ge(deg_ok, g + 2)
                    product(psU, x3T, WS, u_mm)
                if live(t - 3):
                    g = t - 3
                    pe.wait_ge(x2_ok, g + 1)
                    if live(g + 3):
                        pe.wait_ge(adjT_ok, g + 4)
                    turn(psA, x2[(k + 1) % 2], x2T_mm)
                if live(t - 2):
                    g = t - 2
                    pe.wait_ge(sup2_lo, g + 1)
                    product(psC, sup2, adjT[(k + 2) % RING], h2_mm)
                if live(t - 3):
                    g = t - 3
                    pe.wait_ge(x2T_lo, g + 1)
                    if exists(g - 1):
                        pe.wait_ge(z_lo, g)
                    product(psD, x2T, WG, msg_mm)
                if live(t - 1):
                    g = t - 1
                    pe.wait_ge(x1_ok, g + 1)
                    turn(psB[:, 0, :].rearrange("p (t n) -> p t n", t=NT), x1, x1T_mm)
                if live(t):
                    g = t
                    pe.wait_ge(xT_lo, g + 1)
                    product(psX, xT, W0, y_mm, (F + 2, F + 2))
                if live(t - 1):
                    g = t - 1
                    pe.wait_ge(x1T_lo, g + 1)
                    product(psB[:, 1, :].rearrange("p (t n) -> p t n", t=NT), x1T, W1, sup1_mm)
                if live(t - 3):
                    g = t - 3
                    pe.wait_ge(msg_lo, g + 1)
                    product(psD, (linkT[(k + 1) % RING],), msg, agg_mm)
                if live(t):
                    g = t
                    pe.wait_ge(s_ok, g + 1)
                    for rt in range(NT):
                        mm = pe.transpose(s_bcast[:, rt * P:(rt + 1) * P],
                                          s_col[:, rt:rt + 1].broadcast_to([P, P]), ident)
                    mm.then_inc(s_mm, 1)
                if live(t - 2):
                    g = t - 2
                    pe.wait_ge(h2_hi, g + 1)
                    pe.wait_ge(h2_lo, g + 1)
                    product(psC, h2T, W3, sup3_mm)
                if live(t - 4):
                    g = t - 4
                    pe.wait_ge(z_lo, g + 1)
                    pe.wait_ge(u_ok, g + 1)
                    product(psU, adjT[k], z, v_mm)
                if live(t - 1):
                    g = t - 1
                    pe.wait_ge(sup1_lo, g + 1)
                    pe.wait_ge(adj_hi, g + 1)
                    pe.wait_ge(adj_lo, g + 1)
                    product(psB[:, 0, :].rearrange("p (t n) -> p t n", t=NT), sup1, adjT[(k + 3) % RING], h1_mm)
                if live(t - 2):
                    g = t - 2
                    pe.wait_ge(sup3_lo, g + 1)
                    product(psC, adjT[(k + 2) % RING], sup3, o3_mm)
                if live(t):
                    g = t
                    pe.wait_ge(e_hi, g + 1)
                    pe.wait_ge(e_lo, g + 1)
                    if exists(g - 1):
                        pe.wait_ge(h1_full, g)
                    product(psB, eT, y, Ay_mm, (F + 2, F))
                if live(t - 2):
                    g = t - 2
                    pe.wait_ge(link_ok, g + 1)
                    if exists(g - 2):
                        pe.wait_ge(v_ok, g - 1)
                    for rt in range(NT):
                        for ct in range(NT):
                            mm = pe.matmul(psU[:, rt, 0:2], linkT[(k + 2) % RING][:, ct, rt * P:(rt + 1) * P],
                                           ones_r[:], start=(ct == 0), stop=(ct == NT - 1), skip_group_check=True)
                    mm.then_inc(deg_mm, 1)
                if live(t - 3):
                    g = t - 3
                    pe.wait_ge(x3_ok, g + 1)
                    turn(psD, x3[(k + 1) % 2], x3T_mm)
                if live(t - 1):
                    g = t - 1
                    pe.wait_ge(h1_hi, g + 1)
                    pe.wait_ge(h1_lo, g + 1)
                    if exists(g - 1):
                        pe.wait_ge(res_ok[1], g)
                    product(psC, h1T, W2, sup2_mm)
                if live(t - 3):
                    g = t - 3
                    pe.wait_ge(x3T_lo, g + 1)
                    product(psD, x3T, WN, z_mm)

            pe.wait_ge(w_sem, 16 * (N_WLOADS + 1))
            pe.wait_ge(consts_sem, N_CONSTS)
            turn(psC, wc_raw[:, :, 0:F], setup_pe_sem)
            turn(psD, wc_raw[:, :, F:2 * F], setup_pe_sem)
            pe.wait_ge(setup_lo_sem, 7)
            steps(pe, step)

        @block.scalar
        def _(act):
            def copy(dst, src, done):
                act.activation(dst, src, ACT.Identity).then_inc(done, 1)

            def apply_norm(n, dst, g, done):
                act.wait_ge(shift_ok[n], g + 1)
                for rt in range(NT):
                    ins = act.activation(dst[:, rt, :], res[n][:, rt, :], ACT.Identity, bias=shift[n][:, rt:rt + 1],
                                         scale=rstd[n][:, rt:rt + 1])
                ins.then_inc(done, 1)

            def step(t, q, k):
                if live(t):
                    g = t
                    act.wait_ge(xT_mm, g + 1)
                    copy(xT[0][:], psX[:, 0, :].rearrange("p (t n) -> p t n", t=NT), xT_hi)
                    act.wait_ge(adjT_mm, g + 1)
                    if exists(g - 2):
                        act.wait_ge(adj_lo, g - 1)
                    copy(adjT_full[k % 2][:], psA[:], adjT_ok)
                if live(t - 4):
                    g = t - 4
                    act.wait_ge(z_mm, g + 1)
                    copy(z[0][:], psD[:], z_hi)
                if live(t - 1):
                    apply_norm(0, x1, t - 1, x1_ok)
                if live(t - 4):
                    g = t - 4
                    act.wait_ge(u_mm, g + 1)
                    copy(u_self[:], psU[:], u_ok)
                if live(t - 3):
                    g = t - 3
                    act.wait_ge(x2T_mm, g + 1)
                    copy(x2T[0][:], psA[:], x2T_hi)
                if live(t - 2):
                    g = t - 2
                    act.wait_ge(h2_mm, g + 1)
                    for ht in range(NT):
                        ins = act.activation(h2T_full[:, ht, :], psC[:, ht, :], ACT.Relu, bias=b2_col[:, ht:ht + 1])
                    ins.then_inc(h2_full, 1)
                if live(t):
                    g = t
                    act.wait_ge(in_sem[k], 32 * q + 32)
                    if exists(g - 4):
                        act.wait_ge(inv_deg_ok, g - 3)
                    for rt in range(NT):
                        ins = act.activation(unused[:, rt, :], adj_in[k][:, rt, :], ACT.Identity,
                                             accum_out=rowsum[k][:, rt:rt + 1])
                    ins.then_inc(rowsum_ok, 1)
                if live(t - 3):
                    g = t - 3
                    act.wait_ge(msg_mm, g + 1)
                    act.wait_ge(dinv_ok, g + 1)
                    for rt in range(NT):
                        ins = act.activation(msg[0][:, rt, :], psD[:, rt, :], ACT.Identity,
                                             scale=dinv[(k + 1) % 2][:, rt:rt + 1])
                    ins.then_inc(msg_hi, 1)
                if live(t - 1):
                    g = t - 1
                    act.wait_ge(x1T_mm, g + 1)
                    copy(x1T[0][:], psB[:, 0, :].rearrange("p (t n) -> p t n", t=NT), x1T_hi)
                if live(t):
                    g = t
                    act.wait_ge(y_mm, g + 1)
                    copy(y[0][:, :, 0:F], psX[:, :, 0:F], y_hi)
                if live(t - 1):
                    g = t - 1
                    act.wait_ge(sup1_mm, g + 1)
                    copy(sup1[0][:], psB[:, 1, :].rearrange("p (t n) -> p t n", t=NT), sup1_hi)
                if live(t):
                    g = t
                    act.wait_ge(s_mm, g + 1)
                    for rt in range(NT):
                        ins = act.activation(gate[:, rt, :], s_bcast, ACT.Tanh, bias=s_col[:, rt:rt + 1])
                    ins.then_inc(gate_tanh, 1)
                if live(t - 3):
                    g = t - 3
                    act.wait_ge(agg_scaled, g + 1)
                    act.activation(agg[:], agg[:], ACT.Tanh).then_inc(agg_tanh, 1)
                if live(t):
                    g = t
                    act.wait_ge(gate_leaky_ok, g + 1)
                    act.activation(gate[:], gate_leaky[:], ACT.Exp, scale=8.0).then_inc(gate_ok, 1)
                if live(t - 2):
                    g = t - 2
                    act.wait_ge(sup3_mm, g + 1)
                    copy(sup3[0][:], psC[:], sup3_hi)
                if live(t - 1):
                    g = t - 1
                    act.wait_ge(h1_mm, g + 1)
                    for ht in range(NT):
                        ins = act.activation(h1T_full[:, ht, :], psB[:, 0, ht * N:(ht + 1) * N], ACT.Relu,
                                             bias=b1_col[:, ht:ht + 1])
                    ins.then_inc(h1_full, 1)
                if live(t - 3):
                    apply_norm(2, x3[(k + 1) % 2], t - 3, x3_ok)
                if live(t - 4):
                    g = t - 4
                    if exists(g - 2):
                        act.wait_ge(out_sem[k % 2], 8 * (g + 2) - 16 - 8 * (k % 2))
                    apply_norm(3, x4[k % 2], g, x4_ok)
                if live(t - 3):
                    g = t - 3
                    act.wait_ge(x3T_mm, g + 1)
                    copy(x3T[0][:], psD[:], x3T_hi)
                if live(t - 2):
                    apply_norm(1, x2[k % 2], t - 2, x2_ok)
                if live(t - 1):
                    g = t - 1
                    act.wait_ge(sup2_mm, g + 1)
                    copy(sup2[0][:], psC[:], sup2_hi)
                if live(t - 4):
                    g = t - 4
                    act.wait_ge(x4_ok, g + 1)
                    act.dma_start(out_q[q - 1, k], x4[k % 2][:]).then_inc(out_sem[k % 2], 16)

            out_q = out.rearrange("(q k) (t p) f -> q k p t f", k=RING, p=P)
            act.wait_ge(setup_w_sem, 1)
            copy(W0[0][:], w0_raw[:], setup_hi_sem)
            for n, w in (("w1", W1), ("w2", W2), ("w3", W3), ("wg", WG)):
                copy(w[0][:], raws[n][:], setup_hi_sem)
            act.wait_ge(setup_pe_sem, 2)
            copy(WS[0][:], psC[:], setup_hi_sem)
            copy(WN[0][:], psD[:], setup_hi_sem)
            steps(act, step)
            for s in out_sem:
                act.wait_ge(s, 16 * G // 2)

        @block.vector
        def _(dve):
            def rest(dst, full, hi, done):
                dve.tensor_tensor(dst, full, hi.bitcast(F32), ALU.subtract).then_inc(done, 1)

            def norm_stats(n, g):
                dve.wait_ge(res_ok[n], g + 1)
                for rt in range(NT):
                    ins = dve.bn_stats(stats[n][:, rt, :], res[n][:, rt, :])
                ins.then_inc(stats_ok[n], 1)

            def norm_mean_var(n, g):
                dve.wait_ge(stats_ok[n], g + 1)
                dve.memset(wait_pad[:], 0.0)
                for rt in range(NT):
                    ins = dve.bn_aggr(mean_var[n][:, rt, :], stats[n][:, rt, :])
                ins.then_inc(mv_ok[n], 1)

            def step(t, q, k):
                if live(t):
                    g = t
                    dve.wait_ge(xT_hi, g + 1)
                    rest(xT[1][:], psX[:, 0, :].rearrange("p (t n) -> p t n", t=NT), xT[0][:], xT_lo)
                if live(t - 4):
                    g = t - 4
                    dve.wait_ge(z_hi, g + 1)
                    rest(z[1][:], psD[:], z[0][:], z_lo)
                if live(t):
                    g = t
                    dve.wait_ge(adjT_ok, g + 1)
                    dve.scalar_tensor_tensor(out=linkT[k][:], in0=adjT_full[k % 2][:], scalar=0.0, in1=eye[:],
                                             op0=ALU.not_equal, op1=ALU.max).then_inc(link_ok, 1)
                if live(t - 1):
                    g = t - 1
                    dve.wait_ge(rowsum_ok, g + 1)
                    dve.tensor_scalar(deg_floor[:], rowsum[(k + 3) % RING][:], DEG_EPS, None,
                                      ALU.max).then_inc(floor_ok, 1)
                if live(t - 3):
                    g = t - 3
                    dve.wait_ge(x2T_hi, g + 1)
                    rest(x2T[1][:], psA[:], x2T[0][:], x2T_lo)
                if live(t - 1):
                    g = t - 1
                    dve.wait_ge(floor_ok, g + 1)
                    dve.reciprocal(inv_deg[(k + 3) % RING][:], deg_floor[:]).then_inc(inv_deg_ok, 1)
                if live(t - 2):
                    g = t - 2
                    dve.wait_ge(h2_full, g + 1)
                    dve.tensor_copy(h2T[0][:], h2T_full[:]).then_inc(h2_hi, 1)
                if live(t - 3):
                    g = t - 3
                    dve.wait_ge(msg_hi, g + 1)
                    for rt in range(NT):
                        ins = dve.scalar_tensor_tensor(
                            out=msg[1][:, rt, :], in0=psD[:, rt, :], scalar=dinv[(k + 1) % 2][:, rt:rt + 1],
                            in1=msg[0][:, rt, :].bitcast(F32), op0=ALU.mult, op1=ALU.subtract)
                    ins.then_inc(msg_lo, 1)
                if live(t - 1):
                    g = t - 1
                    dve.wait_ge(x1T_hi, g + 1)
                    rest(x1T[1][:], psB[:, 0, :].rearrange("p (t n) -> p t n", t=NT), x1T[0][:], x1T_lo)
                if live(t):
                    g = t
                    dve.wait_ge(y_hi, g + 1)
                    dve.tensor_scalar(s_col[:].rearrange("p (t c) -> p t c", c=1), psX[:, :, F:F + 1], 0.125, None,
                                      ALU.mult)
                    dve.tensor_tensor(y[1][:], psX[:, :, 0:F], y[0][:, :, 0:F].bitcast(F32),
                                      ALU.subtract).then_inc(s_ok, 1)
                if live(t - 1):
                    g = t - 1
                    dve.wait_ge(sup1_hi, g + 1)
                    rest(sup1[1][:], psB[:, 1, :].rearrange("p (t n) -> p t n", t=NT), sup1[0][:], sup1_lo)
                if live(t - 3):
                    g = t - 3
                    dve.wait_ge(agg_mm, g + 1)
                    for rt in range(NT):
                        ins = dve.scalar_tensor_tensor(
                            out=agg[:, rt, :], in0=psD[:, rt, :], scalar=dinv[(k + 1) % 2][:, rt:rt + 1],
                            in1=bg_rows[:, rt, :], op0=ALU.mult, op1=ALU.add)
                    ins.then_inc(agg_scaled, 1)
                if live(t):
                    g = t
                    dve.wait_ge(gate_tanh, g + 1)
                    dve.scalar_tensor_tensor(out=gate_leaky[:], in0=gate[:], scalar=0.1, in1=gate[:],
                                             op0=ALU.mult, op1=ALU.max).then_inc(gate_leaky_ok, 1)
                if live(t - 2):
                    g = t - 2
                    dve.wait_ge(sup3_hi, g + 1)
                    rest(sup3[1][:], psC[:], sup3[0][:], sup3_lo)
                if live(t):
                    g = t
                    dve.wait_ge(gate_ok, g + 1)
                    dve.tensor_tensor(eT_full[:], gate[:], adjT_full[k % 2][:], ALU.mult).then_inc(e_full, 1)
                    dve.wait_ge(e_full, g + 1)
                    dve.tensor_copy(eT[0][:], eT_full[:]).then_inc(e_hi, 1)
                if live(t - 3):
                    norm_stats(2, t - 3)
                if live(t - 4):
                    g = t - 4
                    dve.wait_ge(v_mm, g + 1)
                    dve.wait_ge(u_ok, g + 1)
                    for rt in range(NT):
                        ins = dve.scalar_tensor_tensor(
                            out=pre_relu[:, rt, :], in0=psU[:, rt, :], scalar=inv_deg[k][:, rt:rt + 1],
                            in1=u_self[:, rt, :], op0=ALU.mult, op1=ALU.add)
                    ins.then_inc(v_ok, 1)
                if live(t - 3):
                    norm_mean_var(2, t - 3)
                if live(t - 4):
                    g = t - 4
                    dve.wait_ge(v_ok, g + 1)
                    dve.scalar_tensor_tensor(out=res[3][:], in0=pre_relu[:], scalar=0.0, in1=x3[k % 2][:],
                                             op0=ALU.max, op1=ALU.add).then_inc(res_ok[3], 1)
                if live(t - 1):
                    g = t - 1
                    dve.wait_ge(h1_full, g + 1)
                    dve.tensor_copy(h1T[0][:], h1T_full[:]).then_inc(h1_hi, 1)
                if live(t - 4):
                    norm_stats(3, t - 4)
                if live(t):
                    g = t
                    dve.tensor_copy(adjT[k][0][:], adjT_full[k % 2][:]).then_inc(adj_hi, 1)
                if live(t - 4):
                    norm_mean_var(3, t - 4)
                if live(t - 2):
                    g = t - 2
                    dve.wait_ge(o3_mm, g + 1)
                    dve.wait_ge(x1_b3_ok, g + 1)
                    dve.tensor_tensor(res[1][:], psC[:], x1_b3[k % 2][:], ALU.add).then_inc(res_ok[1], 1)
                    norm_stats(1, g)
                if live(t):
                    g = t
                    dve.wait_ge(Ay_mm, g + 1)
                    dve.reciprocal(inv_esum[:].rearrange("p (t c) -> p t c", c=1),
                                   psB[:, :, F:F + 1]).then_inc(esum_ok, 1)
                if live(t - 2):
                    g = t - 2
                    norm_mean_var(1, g)
                if live(t):
                    g = t
                    dve.wait_ge(esum_ok, g + 1)
                    dve.tensor_tensor(ratio[:], inv_esum[:], rowsum[k][:], ALU.mult).then_inc(ratio_ok, 1)
                if live(t - 2):
                    g = t - 2
                    dve.wait_ge(deg_mm, g + 1)
                    dve.tensor_copy(deg[:].rearrange("p (t c) -> p t c", c=1), psU[:, :, 0:1]).then_inc(deg_ok, 1)
                if live(t):
                    g = t
                    dve.wait_ge(ratio_ok, g + 1)
                    for rt in range(NT):
                        ins = dve.scalar_tensor_tensor(
                            out=res[0][:, rt, :], in0=psB[:, rt, 0:F], scalar=ratio[:, rt:rt + 1],
                            in1=x_in[k][:, rt, :], op0=ALU.mult, op1=ALU.add)
                    ins.then_inc(res_ok[0], 1)
                if live(t - 3):
                    g = t - 3
                    dve.wait_ge(x3T_hi, g + 1)
                    rest(x3T[1][:], psD[:], x3T[0][:], x3T_lo)
                if live(t):
                    norm_stats(0, t)
                if live(t - 1):
                    g = t - 1
                    dve.wait_ge(sup2_hi, g + 1)
                    rest(sup2[1][:], psC[:], sup2[0][:], sup2_lo)
                if live(t):
                    norm_mean_var(0, t)

            dve.memset(ones[:], 1.0).then_inc(consts_sem, 1)
            dve.memset(zero2[:], 0.0).then_inc(consts_sem, 1)
            dve.memset(eps2[:], LN_EPS).then_inc(consts_sem, 1)
            dve.memset(minus_half2[:], -0.5).then_inc(consts_sem, 1)
            dve.wait_ge(consts_sem, 5)
            dve.tensor_copy(ones_r[:], ones[:]).then_inc(consts_sem, 1)
            for rt in range(NT):
                dve.tensor_copy(y[0][:, rt, F:F + 2], ones[:]).then_inc(consts_sem, 1)
            dve.wait_ge(w_sem, 16 * (N_WLOADS + 1))
            for ct in range(NT):
                if ct:
                    dve.wait_ge(wa_sem, ct)
                dve.tensor_tensor_reduce(junk[:], w0_raw[:, ct, 0:F], a_rows[:], 1.0, 0.0, ALU.mult, ALU.add,
                                         wa_col[:, ct:ct + 1]).then_inc(wa_sem, 1)
            dve.wait_ge(wa_sem, NT)
            for c in range(2):
                ins = dve.tensor_copy(w0_raw[:, :, F + c:F + c + 1], wa_col[:].rearrange("p (t c) -> p t c", c=1))
            ins.then_inc(setup_w_sem, 1)
            dve.wait_ge(setup_w_sem, 1)
            for n, (w, full) in enumerate(((W0, w0_raw), (W1, raws["w1"]), (W2, raws["w2"]), (W3, raws["w3"]),
                                           (WG, raws["wg"]), (WS, psC), (WN, psD))):
                dve.wait_ge(setup_hi_sem, n + 1)
                rest(w[1][:], full[:], w[0][:], setup_lo_sem)
            steps(dve, step)

        @block.gpsimd
        def _(pool):
            def norm_scale(n, g):
                pool.wait_ge(mv_ok[n], g + 1)
                pool.tensor_tensor(var_eps[n][:], mean_var[n][:, :, 1], eps2[:], ALU.add)
                pool.tensor_tensor(neg_mean[n][:], zero2[:], mean_var[n][:, :, 0],
                                   ALU.subtract).then_inc(var_ok[n], 1)
                pool.wait_ge(var_ok[n], g + 1)
                if exists(g - 1):
                    pool.wait_ge(applied[n], g)
                pool.tensor_tensor(rstd[n][:], var_eps[n][:], minus_half2[:], ALU.pow).then_inc(rstd_ok[n], 1)
                pool.wait_ge(rstd_ok[n], g + 1)
                pool.tensor_tensor(shift[n][:], neg_mean[n][:], rstd[n][:], ALU.mult).then_inc(shift_ok[n], 1)

            applied = [x1_ok, x2_ok, x3_ok, x4_ok]

            def rest(dst, full, hi, done):
                pool.tensor_tensor(dst, full, hi.bitcast(F32), ALU.subtract).then_inc(done, 1)

            def step(t, q, k):
                if live(t - 1):
                    g = t - 1
                    pool.wait_ge(adj_hi, g + 1)
                    rest(adjT[(k + 3) % RING][1][:], adjT_full[(k + 1) % 2][:], adjT[(k + 3) % RING][0][:], adj_lo)
                    pool.wait_ge(x1_ok, g + 1)
                    if exists(g - 2):
                        pool.wait_ge(res_ok[1], g - 1)
                    pool.tensor_tensor(x1_b3[(k + 1) % 2][:], x1[:], b3_rows[:], ALU.add).then_inc(x1_b3_ok, 1)
                if live(t - 2):
                    g = t - 2
                    pool.wait_ge(h2_hi, g + 1)
                    rest(h2T[1][:], h2T_full[:], h2T[0][:], h2_lo)
                if live(t - 3):
                    g = t - 3
                    pool.wait_ge(agg_tanh, g + 1)
                    pool.tensor_tensor(res[2][:], agg[:], x2[(k + 1) % 2][:], ALU.add).then_inc(res_ok[2], 1)
                if live(t):
                    g = t
                    pool.wait_ge(e_hi, g + 1)
                    rest(eT[1][:], eT_full[:], eT[0][:], e_lo)
                if live(t - 3):
                    norm_scale(2, t - 3)
                if live(t - 1):
                    g = t - 1
                    pool.wait_ge(h1_hi, g + 1)
                    rest(h1T[1][:], h1T_full[:], h1T[0][:], h1_lo)
                if live(t - 4):
                    norm_scale(3, t - 4)
                if live(t - 2):
                    g = t - 2
                    norm_scale(1, g)
                    pool.wait_ge(deg_ok, g + 1)
                    pool.tensor_tensor(dinv[k % 2][:], deg[:], minus_half2[:], ALU.pow).then_inc(dinv_ok, 1)
                if live(t):
                    norm_scale(0, t)

            pool.memset(eye[:], 0.0).then_inc(eye_sem, 1)
            pool.wait_ge(eye_sem, 1)
            pool.affine_select(out=eye[:], in_=eye[:], compare_op=ALU.not_equal, fill=1.0, base=0,
                               pattern=[[P, NT], [-1, N]], channel_multiplier=1).then_inc(consts_sem, 1)
            pool.wait_ge(consts_sem, N_CONSTS)
            steps(pool, step)


_INS = ['x', 'adj', 'L0_gnn_w', 'L0_gnn_a', 'L1_gnn_W1', 'L1_gnn_b1', 'L1_gnn_W2', 'L1_gnn_b2', 'L1_gnn_W3',
        'L1_gnn_b3', 'L2_gnn_W', 'L2_gnn_b', 'L3_gnn_W']


def kernel(**inputs):
    import numpy as _np
    import concourse.bacc as _bacc
    from concourse import mybir as _mybir
    from concourse.bass_utils import run_bass_kernel_spmd as _run

    nc = _bacc.Bacc("TRN2", target_bir_lowering=False, num_devices=1)
    arrays, args = {}, []
    for name in _INS:
        a = _np.ascontiguousarray(inputs[name])
        arrays[f"in_{name}_dram"] = a
        args.append(nc.dram_tensor(f"in_{name}_dram", a.shape, _mybir.dt.from_np(a.dtype), kind="ExternalInput").ap())
    args.append(nc.dram_tensor("out_0_dram", inputs['x'].shape, _mybir.dt.float32, kind="ExternalOutput").ap())
    resnorm_gnn_stack(nc, *args)
    r = _run(nc, [arrays], core_ids=[0])
    return r.results[0]["out_0_dram"]
```

```python
from contextlib import ExitStack

import concourse.bass as bass
from concourse import mybir

P = 128
F32 = mybir.dt.float32
F32R = mybir.dt.float32r
ALU = mybir.AluOpType
ACT = mybir.ActivationFunctionType

LN_EPS = 1e-5
DEG_EPS = 1e-6
RING = 4


def resnorm_gnn_stack(nc, x, adj, w0, a0, w1, b1, w2, b2, w3, b3, wg, bg, wc, out):
    G, N, F = x.shape
    NT = N // P
    assert NT == 2 and F == N
    QUADS = G // RING

    with ExitStack() as ctx:
        def sb(name, shape, dt=F32):
            return ctx.enter_context(nc.sbuf_tensor(name, [P, *shape], dt))

        def split(name, width=F):
            return sb(name + "_hi", [NT, width], F32R), sb(name + "_lo", [NT, width], F32R)

        def sem(name):
            return ctx.enter_context(nc.semaphore(name))

        eye = sb("eye", [NT, N])
        ident = eye[:, 0, 0:P]
        ones = sb("ones", [2])
        ones_r = sb("ones_r", [2], F32R)
        zero2 = sb("zero2", [NT])
        eps2 = sb("eps2", [NT])
        minus_half2 = sb("minus_half2", [NT])
        wait_pad = [sb(f"wait_pad{n}", [1]) for n in range(4)]
        w0_raw = sb("w0_raw", [NT, F + 2])
        wa_col = sb("wa_col", [NT])
        raws = {n: sb(n + "_raw", [NT, F]) for n in ("w1", "w2", "w3", "wg")}
        wc_raw = sb("wc_raw", [NT, 2 * F])
        junk = sb("junk", [F])
        a_rows = sb("a_rows", [F])
        b3_rows = sb("b3_rows", [NT, F])
        bg_rows = sb("bg_rows", [NT, F])
        b1_col = sb("b1_col", [NT])
        b2_col = sb("b2_col", [NT])
        W0 = split("w0", F + 2)
        W1, W2, W3, WG = split("w1"), split("w2"), split("w3"), split("wg")
        WS, WN = split("w_self"), split("w_neigh")

        x_in = [sb(f"x_in{k}", [NT, F]) for k in range(RING)]
        adj_in = [sb(f"adj_in{k}", [NT, N]) for k in range(RING)]
        adjT = [split(f"adjT{k}", N) for k in range(RING)]
        linkT = [sb(f"linkT{k}", [NT, N], F32R) for k in range(RING)]
        rowsum = [sb(f"rowsum{k}", [NT]) for k in range(RING)]
        inv_deg = [sb(f"inv_deg{k}", [NT]) for k in range(RING)]
        adjT_full = [sb(f"adjT_full{k}", [NT, N]) for k in range(2)]
        xT, x1T, x2T, x3T = split("xT"), split("x1T"), split("x2T"), split("x3T")
        y = sb("y_hi", [NT, F + 2], F32R), sb("y_lo", [NT, F], F32R)
        s_col = sb("s_col", [NT])
        gate = sb("gate", [NT, N])
        gate_leaky = sb("gate_leaky", [NT, N])
        unused = sb("unused", [NT, N])
        eT_full = sb("eT_full", [NT, N])
        eT = split("eT", N)
        inv_esum = sb("inv_esum", [NT])
        ratio = sb("ratio", [NT])
        sup1, sup2, sup3 = split("sup1"), split("sup2"), split("sup3")
        h1T_full, h2T_full = sb("h1T_full", [NT, N]), sb("h2T_full", [NT, N])
        h1T, h2T = split("h1T", N), split("h2T", N)
        deg = sb("deg", [NT])
        dinv = [sb(f"dinv{k}", [NT]) for k in range(2)]
        msg = split("msg")
        agg = sb("agg", [NT, F])
        z = split("z")
        u_self = sb("u_self", [NT, F])
        pre_relu = sb("pre_relu", [NT, F])
        deg_floor = sb("deg_floor", [NT])
        res = [sb(f"res{n}", [NT, F]) for n in range(4)]
        x1 = sb("x1", [NT, F])
        x1_b3 = [sb(f"x1_b3_{k}", [NT, F]) for k in range(2)]
        x2 = [sb(f"x2_{k}", [NT, F]) for k in range(2)]
        x3 = [sb(f"x3_{k}", [NT, F]) for k in range(2)]
        x4 = [sb(f"x4_{k}", [NT, F]) for k in range(RING)]
        stats = [sb(f"stats{n}", [NT, 6]) for n in range(4)]
        mean_var = [sb(f"mean_var{n}", [NT, 2]) for n in range(4)]
        var_eps = [sb(f"var_eps{n}", [NT]) for n in range(4)]
        neg_mean = [sb(f"neg_mean{n}", [NT]) for n in range(4)]
        rstd = [sb(f"rstd{n}", [NT]) for n in range(4)]
        shift = [sb(f"shift{n}", [NT]) for n in range(4)]

        BANK = 512
        psX = ctx.enter_context(nc.psum_tensor("psX", [P, 2, BANK], F32))
        psB = ctx.enter_context(nc.psum_tensor("psB", [P, 2, BANK], F32))
        psA, psC, psD, psU = (ctx.enter_context(nc.psum_tensor(n, [P, NT, F], F32)) for n in ("psA", "psC", "psD", "psU"))
        s_bcast = psX[:, 0, 0:N]

        x_loaded = [sem(f"x_loaded{k}") for k in range(RING)]
        adj_loaded = [sem(f"adj_loaded{k}") for k in range(RING)]
        stored = [sem(f"stored{k}") for k in range(RING)]
        WEIGHTS = ("w0", "w1", "w2", "w3", "wg", "wc")
        w_in = {n: sem(n + "_loaded") for n in WEIGHTS}
        w_hi = {n: sem(n + "_hi_ready") for n in WEIGHTS}
        w_lo = {n: sem(n + "_lo_ready") for n in WEIGHTS}
        biases_loaded, consts_ready, w0_widened, wc_turned, wa_ready, eye_cleared = (
            sem(n) for n in ("biases_loaded", "consts_ready", "w0_widened", "wc_turned", "wa_ready", "eye_cleared"))
        (xT_mm, adjT_mm, y_mm, s_mm, Ay_mm, x1T_mm, sup1_mm, h1_mm, sup2_mm, h2_mm, sup3_mm, o3_mm, deg_mm,
         x2T_mm, msg_mm, agg_mm, x3T_mm, z_mm, u_mm, v_mm) = (
            sem(n) for n in ("xT_mm", "adjT_mm", "y_mm", "s_mm", "Ay_mm", "x1T_mm", "sup1_mm", "h1_mm",
                "sup2_mm", "h2_mm", "sup3_mm", "o3_mm", "deg_mm", "x2T_mm", "msg_mm", "agg_mm", "x3T_mm",
                "z_mm", "u_mm", "v_mm"))
        (xT_hi, adjT_ok, rowsum_ok, y_hi, gate_tanh, gate_ok, x2_ok, x3_ok, x1T_hi, sup1_hi, h1_full, sup2_hi,
         h2_full, sup3_hi, x2T_hi, msg_hi, agg_tanh, x3T_hi, z_hi, u_ok, adj_hi, h1_hi, h2_hi, relu_ok) = (
            sem(n) for n in ("xT_hi", "adjT_ok", "rowsum_ok", "y_hi", "gate_tanh", "gate_ok", "x2_ok", "x3_ok",
                "x1T_hi", "sup1_hi", "h1_full", "sup2_hi", "h2_full", "sup3_hi", "x2T_hi", "msg_hi", "agg_tanh",
                "x3T_hi", "z_hi", "u_ok", "adj_hi", "h1_hi", "h2_hi", "relu_ok"))
        (x1_ok, x4_ok, xT_lo, link_ok, gate_leaky_ok, s_ok, e_full, e_hi, e_lo, x1T_lo, sup1_lo, sup2_lo,
         sup3_lo, x2T_lo, msg_lo, agg_scaled, x3T_lo, z_lo, inv_deg_ok, v_ok, deg_ok, esum_ok, ratio_ok,
         floor_ok) = (
            sem(n) for n in ("x1_ok", "x4_ok", "xT_lo", "link_ok", "gate_leaky_ok", "s_ok", "e_full", "e_hi",
                "e_lo", "x1T_lo", "sup1_lo", "sup2_lo", "sup3_lo", "x2T_lo", "msg_lo", "agg_scaled", "x3T_lo",
                "z_lo", "inv_deg_ok", "v_ok", "deg_ok", "esum_ok", "ratio_ok", "floor_ok"))
        (h1_lo, h2_lo, adj_lo, dinv_ok, x1_b3_ok) = (
            sem(n) for n in ("h1_lo", "h2_lo", "adj_lo", "dinv_ok", "x1_b3_ok"))

        res_ok = [sem(f"res_ok{n}") for n in range(4)]
        stats_ok = [sem(f"stats_ok{n}") for n in range(4)]
        mean_var_ok = [sem(f"mean_var_ok{n}") for n in range(4)]
        var_ok = [sem(f"var_ok{n}") for n in range(4)]
        rstd_ok = [sem(f"rstd_ok{n}") for n in range(4)]
        shift_ok = [sem(f"shift_ok{n}") for n in range(4)]

        N_BIASES = 2 + 2 * NT
        N_CONSTS = 8
        block = ctx.enter_context(nc.Block())

        def steps(eng, step, setup=None):
            for k in range(RING):
                if setup and k in setup:
                    setup[k]()
                step(k, 0, k)
            with eng.Fori(1, QUADS) as q:
                for k in range(RING):
                    step(q * RING + k, q, k)
            for k in range(RING):
                step(G + k, QUADS, k)

        def live(g):
            return not isinstance(g, int) or 0 <= g < G

        def first(g):
            return isinstance(g, int) and g == 0

        def tiles(bank):
            return bank.rearrange("p (t n) -> p t n", t=NT)

        @block.sync
        def _(sp):
            def load(q, k):
                sp.dma_start(x_in[k][:], x_q[q, k]).then_inc(x_loaded[k], 16)
                sp.dma_start(adj_in[k][:], adj_q[q, k]).then_inc(adj_loaded[k], 16)

            x_q = x.rearrange("(q k) (t p) f -> q k p t f", k=RING, p=P)
            adj_q = adj.rearrange("(q k) (t p) f -> q k p t f", k=RING, p=P)

            out_q = out.rearrange("(q k) (t p) f -> q k p t f", k=RING, p=P)

            def rows(v):
                return v.rearrange("(a f) -> a f", a=1).broadcast_to([P, F])

            def cols(v):
                return v.rearrange("(t p) -> p t", p=P)

            def weight(n, dst, src):
                sp.dma_start(dst, src.rearrange("(t p) h -> p t h", p=P)).then_inc(w_in[n], 16)

            sp.dma_start(x_in[0][:], x_q[0, 0]).then_inc(x_loaded[0], 16)
            weight("w0", w0_raw[:, :, 0:F], w0)
            sp.dma_start(a_rows[:], rows(a0)).then_inc(w_in["w0"], 16)
            sp.dma_start(adj_in[0][:], adj_q[0, 0]).then_inc(adj_loaded[0], 16)
            weight("w1", raws["w1"][:], w1)
            load(0, 1)
            with nc.allow_non_contiguous_dma(reason="two short columns, once"):
                sp.dma_start(b1_col[:], cols(b1)).then_inc(biases_loaded, 16)
                sp.dma_start(b2_col[:], cols(b2)).then_inc(biases_loaded, 16)
            for t in range(NT):
                sp.dma_start(b3_rows[:, t, :], rows(b3)).then_inc(biases_loaded, 16)
                sp.dma_start(bg_rows[:, t, :], rows(bg)).then_inc(biases_loaded, 16)
            weight("w2", raws["w2"][:], w2)
            weight("w3", raws["w3"][:], w3)
            weight("wc", wc_raw[:], wc)
            load(0, 2)
            weight("wg", raws["wg"][:], wg)
            load(0, 3)

            def reload(q, k):
                g = q * RING + k - RING
                sp.wait_ge(adjT_mm, g + 1)
                sp.wait_ge(rowsum_ok, g + 1)
                sp.wait_ge(res_ok[0], g + 1)
                load(q, k)

            def store(q, k):
                sp.wait_ge(x4_ok, q * RING + k + 1)
                sp.dma_start(out_q[q, k], x4[k][:]).then_inc(stored[k], 16)

            for k in range(RING):
                reload(1, k)
            with sp.Fori(2, QUADS) as q:
                for k in range(RING):
                    reload(q, k)
                    store(q - 2, k)
            for q in (QUADS - 2, QUADS - 1):
                for k in range(RING):
                    store(q, k)
            for k in range(RING):
                sp.wait_ge(stored[k], 16 * QUADS + 1)

        @block.tensor
        def _(pe):
            def turn(dst, src, done):
                for rt in range(NT):
                    for ct in range(NT):
                        mm = pe.transpose(dst[:, ct, rt * P:(rt + 1) * P], src[:, rt, ct * P:(ct + 1) * P], ident)
                mm.then_inc(done, 1)

            def product(dst, left, right, done, widths=(F, F)):
                passes = [(l, r) for l in range(len(left)) for r in range(len(right)) if l + r < 2]
                for rt in range(NT):
                    n = 0
                    for ct in range(NT):
                        for l, r in passes:
                            w = widths[r]
                            mm = pe.matmul(dst[:, rt, 0:w], left[l][:, ct, rt * P:(rt + 1) * P],
                                           right[r][:, ct, 0:w], start=(n == 0), stop=(n == NT * len(passes) - 1),
                                           skip_group_check=True)
                            n += 1
                mm.then_inc(done, 1)

            def step(t, q, k):
                if live(t - 2):
                    g, slot = t - 2, (k - 2) % RING
                    pe.wait_ge(x1T_lo, g + 1)
                    if first(g):
                        pe.wait_ge(w_lo["w1"], 1)
                    product(tiles(psB[:, 1, :]), x1T, W1, sup1_mm)
                if live(t - 3):
                    g, slot = t - 3, (k - 3) % RING
                    pe.wait_ge(h2_hi, g + 1)
                    pe.wait_ge(h2_lo, g + 1)
                    if first(g):
                        pe.wait_ge(w_lo["w3"], 1)
                    product(psC, h2T, W3, sup3_mm)
                    pe.wait_ge(link_ok, g + 1)
                    if live(g - 2):
                        pe.wait_ge(v_ok, g - 1)
                    for rt in range(NT):
                        for ct in range(NT):
                            mm = pe.matmul(psU[:, rt, 0:2], linkT[slot][:, ct, rt * P:(rt + 1) * P],
                                           ones_r[:], start=(ct == 0), stop=(ct == NT - 1), skip_group_check=True)
                    mm.then_inc(deg_mm, 1)
                if live(t - 2):
                    g, slot = t - 2, (k - 2) % RING
                    pe.wait_ge(sup1_lo, g + 1)
                    pe.wait_ge(adj_hi, g + 1)
                    pe.wait_ge(adj_lo, g + 1)
                    product(tiles(psB[:, 0, :]), sup1, adjT[slot], h1_mm)
                if live(t):
                    g, slot = t, k
                    pe.wait_ge(x_loaded[slot], 16 * q + 16)
                    if live(g - 1):
                        pe.wait_ge(gate_tanh, g)
                    turn(tiles(psX[:, 0, :]), x_in[slot], xT_mm)
                if live(t - 3):
                    g, slot = t - 3, (k - 3) % RING
                    pe.wait_ge(sup3_lo, g + 1)
                    product(psC, adjT[slot], sup3, o3_mm)
                if live(t):
                    g, slot = t, k
                    pe.wait_ge(adj_loaded[slot], 16 * q + 16)
                    if live(g - 4):
                        pe.wait_ge(x2T_lo, g - 3)
                    turn(psA, adj_in[slot], adjT_mm)
                if live(t - 4):
                    g, slot = t - 4, (k - 4) % RING
                    pe.wait_ge(x3_ok, g + 1)
                    turn(psD, x3[slot % 2], x3T_mm)
                if live(t - 1):
                    g, slot = t - 1, (k - 1) % RING
                    pe.wait_ge(e_hi, g + 1)
                    pe.wait_ge(e_lo, g + 1)
                    pe.wait_ge(s_ok, g + 1)
                    if live(g - 1):
                        pe.wait_ge(h1_full, g)
                    product(psB, eT, y, Ay_mm, (F + 2, F))
                if live(t - 2):
                    g, slot = t - 2, (k - 2) % RING
                    pe.wait_ge(h1_hi, g + 1)
                    pe.wait_ge(h1_lo, g + 1)
                    if live(g - 1):
                        pe.wait_ge(res_ok[1], g)
                    if first(g):
                        pe.wait_ge(w_lo["w2"], 1)
                    product(psC, h1T, W2, sup2_mm)
                if live(t - 4):
                    g, slot = t - 4, (k - 4) % RING
                    pe.wait_ge(x3T_lo, g + 1)
                    if first(g):
                        pe.wait_ge(w_lo["wc"], 2)
                    product(psD, x3T, WN, z_mm)
                if live(t - 3):
                    g, slot = t - 3, (k - 3) % RING
                    pe.wait_ge(x2_ok, g + 1)
                    if live(g + 3):
                        pe.wait_ge(adjT_ok, g + 4)
                    turn(psA, x2[slot % 2], x2T_mm)
                if live(t - 4):
                    g, slot = t - 4, (k - 4) % RING
                    pe.wait_ge(x3T_lo, g + 1)
                    if live(g + 1):
                        pe.wait_ge(deg_ok, g + 2)
                    if isinstance(g, int) and g >= 1:
                        pe.wait_ge(v_ok, g)
                    if first(g):
                        pe.wait_ge(w_lo["wc"], 2)
                    product(psU, x3T, WS, u_mm)
                if live(t - 2):
                    g, slot = t - 2, (k - 2) % RING
                    pe.wait_ge(sup2_lo, g + 1)
                    product(psC, sup2, adjT[slot], h2_mm)
                if live(t - 3):
                    g, slot = t - 3, (k - 3) % RING
                    pe.wait_ge(x2T_lo, g + 1)
                    if live(g - 1):
                        pe.wait_ge(z_lo, g)
                    if first(g):
                        pe.wait_ge(w_lo["wg"], 1)
                    product(psD, x2T, WG, msg_mm)
                if live(t):
                    g, slot = t, k
                    pe.wait_ge(xT_lo, g + 1)
                    if first(g):
                        pe.wait_ge(w_lo["w0"], 1)
                    product(psX, xT, W0, y_mm, (F + 2, F + 2))
                if live(t - 1):
                    g, slot = t - 1, (k - 1) % RING
                    pe.wait_ge(x1_ok, g + 1)
                    turn(tiles(psB[:, 0, :]), x1, x1T_mm)
                if live(t - 4):
                    g, slot = t - 4, (k - 4) % RING
                    pe.wait_ge(z_lo, g + 1)
                    pe.wait_ge(u_ok, g + 1)
                    product(psU, adjT[slot], z, v_mm)
                if live(t - 3):
                    g, slot = t - 3, (k - 3) % RING
                    pe.wait_ge(msg_lo, g + 1)
                    product(psD, (linkT[slot],), msg, agg_mm)
                if live(t):
                    g, slot = t, k
                    pe.wait_ge(s_ok, g + 1)
                    for rt in range(NT):
                        mm = pe.transpose(s_bcast[:, rt * P:(rt + 1) * P],
                                          s_col[:, rt:rt + 1].broadcast_to([P, P]), ident)
                    mm.then_inc(s_mm, 1)

            def turn_wc():
                pe.wait_ge(w_in["wc"], 16)
                turn(psD, wc_raw[:, :, 0:F], wc_turned)
                turn(psU, wc_raw[:, :, F:2 * F], wc_turned)

            pe.wait_ge(consts_ready, N_CONSTS)
            steps(pe, step, {1: turn_wc})

        @block.scalar
        def _(act):
            def copy(dst, src, done):
                act.activation(dst, src, ACT.Identity).then_inc(done, 1)

            def apply_norm(n, dst, done):
                for rt in range(NT):
                    ins = act.activation(dst[:, rt, :], res[n][:, rt, :], ACT.Identity, bias=shift[n][:, rt:rt + 1],
                                         scale=rstd[n][:, rt:rt + 1])
                ins.then_inc(done, 1)

            def step(t, q, k):
                if live(t - 3):
                    g, slot = t - 3, (k - 3) % RING
                    act.wait_ge(sup3_mm, g + 1)
                    if live(g - 1):
                        act.wait_ge(o3_mm, g)
                    copy(sup3[0][:], psC[:], sup3_hi)
                if live(t - 1):
                    g, slot = t - 1, (k - 1) % RING
                    act.wait_ge(adj_loaded[slot], 16 * (q + (k - 1) // RING) + 16)
                    for rt in range(NT):
                        ins = act.activation(unused[:, rt, :], adj_in[slot][:, rt, :], ACT.Identity,
                                             accum_out=rowsum[slot][:, rt:rt + 1])
                    ins.then_inc(rowsum_ok, 1)
                if live(t - 2):
                    g, slot = t - 2, (k - 2) % RING
                    act.wait_ge(h1_mm, g + 1)
                    if live(g - 1):
                        act.wait_ge(h1_lo, g)
                    if first(g):
                        act.wait_ge(biases_loaded, 16 * N_BIASES)
                    for ht in range(NT):
                        ins = act.activation(h1T_full[:, ht, :], psB[:, 0, ht * N:(ht + 1) * N], ACT.Relu,
                                             bias=b1_col[:, ht:ht + 1])
                    ins.then_inc(h1_full, 1)
                if live(t - 4):
                    g, slot = t - 4, (k - 4) % RING
                    act.wait_ge(shift_ok[2], g + 1)
                    apply_norm(2, x3[slot % 2], x3_ok)
                if live(t - 2):
                    g, slot = t - 2, (k - 2) % RING
                    act.wait_ge(h1_full, g + 1)
                    if live(g - 1):
                        act.wait_ge(sup2_mm, g)
                    copy(h1T[0][:], h1T_full[:], h1_hi)
                if live(t - 4):
                    g, slot = t - 4, (k - 4) % RING
                    act.wait_ge(x3T_mm, g + 1)
                    copy(x3T[0][:], psD[:], x3T_hi)
                if live(t):
                    g, slot = t, k
                    act.wait_ge(xT_mm, g + 1)
                    if live(g - 1):
                        act.wait_ge(y_mm, g)
                    copy(xT[0][:], tiles(psX[:, 0, :]), xT_hi)
                    act.wait_ge(adjT_mm, g + 1)
                    if live(g - 2):
                        act.wait_ge(adj_lo, g - 1)
                    if live(g - 2):
                        act.wait_ge(e_full, g - 1)
                    if live(g - 2):
                        act.wait_ge(link_ok, g - 1)
                    copy(adjT_full[slot % 2][:], psA[:], adjT_ok)
                if live(t - 1):
                    g, slot = t - 1, (k - 1) % RING
                    act.wait_ge(adjT_ok, g + 1)
                    copy(adjT[slot][0][:], adjT_full[slot % 2][:], adj_hi)
                if live(t - 3):
                    g, slot = t - 3, (k - 3) % RING
                    act.wait_ge(shift_ok[1], g + 1)
                    apply_norm(1, x2[slot % 2], x2_ok)
                if live(t - 2):
                    g, slot = t - 2, (k - 2) % RING
                    act.wait_ge(sup2_mm, g + 1)
                    if live(g - 1):
                        act.wait_ge(h2_mm, g)
                    copy(sup2[0][:], psC[:], sup2_hi)
                if live(t - 4):
                    g, slot = t - 4, (k - 4) % RING
                    act.wait_ge(z_mm, g + 1)
                    copy(z[0][:], psD[:], z_hi)
                if live(t - 3):
                    g, slot = t - 3, (k - 3) % RING
                    act.wait_ge(x2T_mm, g + 1)
                    if live(g - 1):
                        act.wait_ge(msg_mm, g)
                    copy(x2T[0][:], psA[:], x2T_hi)
                if live(t - 2):
                    g, slot = t - 2, (k - 2) % RING
                    act.wait_ge(h2_mm, g + 1)
                    if live(g - 1):
                        act.wait_ge(h2_lo, g)
                    if first(g):
                        act.wait_ge(biases_loaded, 16 * N_BIASES)
                    for ht in range(NT):
                        ins = act.activation(h2T_full[:, ht, :], psC[:, ht, :], ACT.Relu,
                                             bias=b2_col[:, ht:ht + 1])
                    ins.then_inc(h2_full, 1)
                if live(t - 4):
                    g, slot = t - 4, (k - 4) % RING
                    act.wait_ge(u_mm, g + 1)
                    copy(u_self[:], psU[:], u_ok)
                if live(t - 3):
                    g, slot = t - 3, (k - 3) % RING
                    act.wait_ge(msg_mm, g + 1)
                    act.wait_ge(dinv_ok, g + 1)
                    if live(g - 1):
                        act.wait_ge(agg_mm, g)
                    for rt in range(NT):
                        ins = act.activation(msg[0][:, rt, :], psD[:, rt, :], ACT.Identity,
                                             scale=dinv[slot % 2][:, rt:rt + 1])
                    ins.then_inc(msg_hi, 1)
                if live(t - 2):
                    g, slot = t - 2, (k - 2) % RING
                    act.wait_ge(h2_full, g + 1)
                    if live(g - 1):
                        act.wait_ge(sup3_mm, g)
                    copy(h2T[0][:], h2T_full[:], h2_hi)
                if live(t):
                    g, slot = t, k
                    act.wait_ge(y_mm, g + 1)
                    if live(g - 1):
                        act.wait_ge(Ay_mm, g)
                    copy(y[0][:, :, 0:F], psX[:, :, 0:F], y_hi)
                if live(t - 1):
                    g, slot = t - 1, (k - 1) % RING
                    act.wait_ge(x1T_mm, g + 1)
                    if live(g - 1):
                        act.wait_ge(sup1_mm, g)
                    copy(x1T[0][:], tiles(psB[:, 0, :]), x1T_hi)
                if live(t):
                    g, slot = t, k
                    act.wait_ge(s_mm, g + 1)
                    if live(g - 1):
                        act.wait_ge(e_full, g)
                    for rt in range(NT):
                        ins = act.activation(gate[:, rt, :], s_bcast, ACT.Tanh, bias=s_col[:, rt:rt + 1])
                    ins.then_inc(gate_tanh, 1)
                if live(t - 3):
                    g, slot = t - 3, (k - 3) % RING
                    act.wait_ge(agg_scaled, g + 1)
                    act.activation(agg[:], agg[:], ACT.Tanh).then_inc(agg_tanh, 1)
                if live(t - 1):
                    g, slot = t - 1, (k - 1) % RING
                    act.wait_ge(sup1_mm, g + 1)
                    if live(g - 1):
                        act.wait_ge(h1_mm, g)
                    copy(sup1[0][:], tiles(psB[:, 1, :]), sup1_hi)
                if live(t - 4):
                    g, slot = t - 4, (k - 4) % RING
                    act.wait_ge(v_ok, g + 1)
                    act.activation(pre_relu[:], pre_relu[:], ACT.Relu).then_inc(relu_ok, 1)
                if live(t):
                    g, slot = t, k
                    act.wait_ge(gate_leaky_ok, g + 1)
                    act.activation(gate[:], gate_leaky[:], ACT.Exp, scale=8.0).then_inc(gate_ok, 1)


            def round_w1_w2():
                act.wait_ge(w_in["w1"], 16)
                copy(W1[0][:], raws["w1"][:], w_hi["w1"])
                act.wait_ge(w_in["w2"], 16)
                copy(W2[0][:], raws["w2"][:], w_hi["w2"])

            def round_others():
                act.wait_ge(w_in["w3"], 16)
                copy(W3[0][:], raws["w3"][:], w_hi["w3"])
                act.wait_ge(w_in["wg"], 16)
                copy(WG[0][:], raws["wg"][:], w_hi["wg"])
                act.wait_ge(wc_turned, 2)
                copy(WS[0][:], psD[:], w_hi["wc"])
                copy(WN[0][:], psU[:], w_hi["wc"])

            act.wait_ge(w0_widened, 1)
            copy(W0[0][:], w0_raw[:], w_hi["w0"])
            steps(act, step, {1: round_w1_w2, 2: round_others})

        @block.vector
        def _(dve):
            def copy(dst, src, done):
                dve.tensor_copy(dst, src).then_inc(done, 1)

            def rest(dst, full, hi, done):
                dve.tensor_tensor(dst, full, hi.bitcast(F32), ALU.subtract).then_inc(done, 1)

            def apply_norm(n, dst, done):
                for rt in range(NT):
                    ins = dve.tensor_scalar(dst[:, rt, :], res[n][:, rt, :], mean_var[n][:, rt, 0:1],
                                            rstd[n][:, rt:rt + 1], ALU.subtract, ALU.mult)
                ins.then_inc(done, 1)

            def norm_stats(n, g):
                dve.wait_ge(res_ok[n], g + 1)
                for rt in range(NT):
                    ins = dve.bn_stats(stats[n][:, rt, :], res[n][:, rt, :])
                ins.then_inc(stats_ok[n], 1)

            def norm_mean_var(n):
                dve.memset(wait_pad[n][:], 0.0)
                for rt in range(NT):
                    ins = dve.bn_aggr(mean_var[n][:, rt, :], stats[n][:, rt, :])
                ins.then_inc(mean_var_ok[n], 1)

            def step(t, q, k):
                if live(t - 4):
                    g, slot = t - 4, (k - 4) % RING
                    dve.wait_ge(rowsum_ok, g + 1)
                    dve.tensor_scalar(deg_floor[:], rowsum[slot][:], DEG_EPS, None, ALU.max).then_inc(floor_ok, 1)
                    dve.wait_ge(floor_ok, g + 1)
                    dve.reciprocal(inv_deg[slot][:], deg_floor[:]).then_inc(inv_deg_ok, 1)
                if live(t):
                    g, slot = t, k
                    dve.wait_ge(xT_hi, g + 1)
                    if live(g - 1):
                        dve.wait_ge(y_mm, g)
                    rest(xT[1][:], tiles(psX[:, 0, :]), xT[0][:], xT_lo)
                if live(t - 1):
                    g, slot = t - 1, (k - 1) % RING
                    dve.wait_ge(rstd_ok[0], g + 1)
                    if live(g - 1):
                        dve.wait_ge(x1T_mm, g)
                    if live(g - 1):
                        dve.wait_ge(x1_b3_ok, g)
                    apply_norm(0, x1, x1_ok)
                    dve.wait_ge(adjT_ok, g + 1)
                    dve.scalar_tensor_tensor(out=linkT[slot][:], in0=adjT_full[slot % 2][:], scalar=0.0, in1=eye[:],
                                             op0=ALU.not_equal, op1=ALU.max).then_inc(link_ok, 1)
                if live(t - 3):
                    g, slot = t - 3, (k - 3) % RING
                    dve.wait_ge(msg_hi, g + 1)
                    for rt in range(NT):
                        ins = dve.scalar_tensor_tensor(
                            out=msg[1][:, rt, :], in0=psD[:, rt, :], scalar=dinv[slot % 2][:, rt:rt + 1],
                            in1=msg[0][:, rt, :].bitcast(F32), op0=ALU.mult, op1=ALU.subtract)
                    ins.then_inc(msg_lo, 1)
                if live(t):
                    g, slot = t, k
                    dve.wait_ge(y_hi, g + 1)
                    if live(g - 1):
                        dve.wait_ge(Ay_mm, g)
                    if live(g - 1):
                        dve.wait_ge(gate_tanh, g)
                    dve.tensor_scalar(s_col[:].rearrange("p (t c) -> p t c", c=1), psX[:, :, F:F + 1], 0.125, None,
                                      ALU.mult)
                    dve.tensor_tensor(y[1][:], psX[:, :, 0:F], y[0][:, :, 0:F].bitcast(F32), ALU.subtract).then_inc(s_ok, 1)
                if live(t - 1):
                    g, slot = t - 1, (k - 1) % RING
                    dve.wait_ge(x1T_hi, g + 1)
                    rest(x1T[1][:], tiles(psB[:, 0, :]), x1T[0][:], x1T_lo)
                if live(t - 3):
                    g, slot = t - 3, (k - 3) % RING
                    dve.wait_ge(agg_mm, g + 1)
                    if live(g - 1):
                        dve.wait_ge(res_ok[2], g)
                    if first(g):
                        dve.wait_ge(biases_loaded, 16 * N_BIASES)
                    for rt in range(NT):
                        ins = dve.scalar_tensor_tensor(
                            out=agg[:, rt, :], in0=psD[:, rt, :], scalar=dinv[slot % 2][:, rt:rt + 1],
                            in1=bg_rows[:, rt, :], op0=ALU.mult, op1=ALU.add)
                    ins.then_inc(agg_scaled, 1)
                if live(t - 4):
                    g, slot = t - 4, (k - 4) % RING
                    dve.wait_ge(v_mm, g + 1)
                    dve.wait_ge(u_ok, g + 1)
                    dve.wait_ge(inv_deg_ok, g + 1)
                    for rt in range(NT):
                        ins = dve.scalar_tensor_tensor(
                            out=pre_relu[:, rt, :], in0=psU[:, rt, :], scalar=inv_deg[slot][:, rt:rt + 1],
                            in1=u_self[:, rt, :], op0=ALU.mult, op1=ALU.add)
                    ins.then_inc(v_ok, 1)
                if live(t):
                    g, slot = t, k
                    dve.wait_ge(gate_tanh, g + 1)
                    if live(g - 1):
                        dve.wait_ge(gate_ok, g)
                    dve.scalar_tensor_tensor(out=gate_leaky[:], in0=gate[:], scalar=0.1, in1=gate[:],
                                             op0=ALU.mult, op1=ALU.max).then_inc(gate_leaky_ok, 1)
                if live(t - 1):
                    g, slot = t - 1, (k - 1) % RING
                    dve.wait_ge(sup1_hi, g + 1)
                    rest(sup1[1][:], tiles(psB[:, 1, :]), sup1[0][:], sup1_lo)
                if live(t - 3):
                    g, slot = t - 3, (k - 3) % RING
                    norm_stats(2, g)
                    dve.wait_ge(stats_ok[2], g + 1)
                    if live(g - 1):
                        dve.wait_ge(shift_ok[2], g)
                    norm_mean_var(2)
                if live(t - 2):
                    g, slot = t - 2, (k - 2) % RING
                    dve.wait_ge(sup3_hi, g + 1)
                    rest(sup3[1][:], psC[:], sup3[0][:], sup3_lo)
                if live(t):
                    g, slot = t, k
                    dve.wait_ge(gate_ok, g + 1)
                    dve.wait_ge(adjT_ok, g + 1)
                    dve.tensor_tensor(eT_full[:], gate[:], adjT_full[slot % 2][:], ALU.mult).then_inc(e_full, 1)
                    dve.wait_ge(e_full, g + 1)
                    if live(g - 1):
                        dve.wait_ge(Ay_mm, g)
                    copy(eT[0][:], eT_full[:], e_hi)
                    dve.wait_ge(e_hi, g + 1)
                    if live(g - 1):
                        dve.wait_ge(Ay_mm, g)
                    rest(eT[1][:], eT_full[:], eT[0][:], e_lo)
                if live(t - 2):
                    g, slot = t - 2, (k - 2) % RING
                    dve.wait_ge(o3_mm, g + 1)
                    dve.wait_ge(x1_b3_ok, g + 1)
                    if live(g - 1):
                        dve.wait_ge(x2_ok, g)
                    dve.tensor_tensor(res[1][:], psC[:], x1_b3[slot % 2][:], ALU.add).then_inc(res_ok[1], 1)
                    norm_stats(1, g)
                    dve.wait_ge(stats_ok[1], g + 1)
                    if live(g - 1):
                        dve.wait_ge(shift_ok[1], g)
                    norm_mean_var(1)
                if live(t - 3):
                    g, slot = t - 3, (k - 3) % RING
                    dve.wait_ge(x3T_hi, g + 1)
                    rest(x3T[1][:], psD[:], x3T[0][:], x3T_lo)
                if live(t):
                    g, slot = t, k
                    dve.wait_ge(Ay_mm, g + 1)
                    dve.reciprocal(inv_esum[:].rearrange("p (t c) -> p t c", c=1), psB[:, :, F:F + 1]).then_inc(esum_ok, 1)
                    dve.wait_ge(esum_ok, g + 1)
                    dve.wait_ge(rowsum_ok, g + 1)
                    dve.tensor_tensor(ratio[:], inv_esum[:], rowsum[slot][:], ALU.mult).then_inc(ratio_ok, 1)
                    dve.wait_ge(ratio_ok, g + 1)
                    for rt in range(NT):
                        ins = dve.scalar_tensor_tensor(
                            out=res[0][:, rt, :], in0=psB[:, rt, 0:F], scalar=ratio[:, rt:rt + 1],
                            in1=x_in[slot][:, rt, :], op0=ALU.mult, op1=ALU.add)
                    ins.then_inc(res_ok[0], 1)
                if live(t - 4):
                    g, slot = t - 4, (k - 4) % RING
                    norm_stats(3, g)
                    dve.wait_ge(stats_ok[3], g + 1)
                    norm_mean_var(3)
                if live(t - 2):
                    g, slot = t - 2, (k - 2) % RING
                    dve.wait_ge(deg_mm, g + 1)
                    if live(g - 1):
                        dve.wait_ge(dinv_ok, g)
                    dve.tensor_copy(deg[:].rearrange("p (t c) -> p t c", c=1), psU[:, :, 0:1]).then_inc(deg_ok, 1)
                if live(t):
                    g, slot = t, k
                    norm_stats(0, g)
                    dve.wait_ge(stats_ok[0], g + 1)
                    if live(g - 1):
                        dve.wait_ge(rstd_ok[0], g)
                    norm_mean_var(0)
                if live(t - 1):
                    g, slot = t - 1, (k - 1) % RING
                    dve.wait_ge(sup2_hi, g + 1)
                    rest(sup2[1][:], psC[:], sup2[0][:], sup2_lo)
                if live(t - 3):
                    g, slot = t - 3, (k - 3) % RING
                    dve.wait_ge(z_hi, g + 1)
                    rest(z[1][:], psD[:], z[0][:], z_lo)
                if live(t - 2):
                    g, slot = t - 2, (k - 2) % RING
                    dve.wait_ge(x2T_hi, g + 1)
                    rest(x2T[1][:], psA[:], x2T[0][:], x2T_lo)
                if live(t - 4):
                    g, slot = t - 4, (k - 4) % RING
                    dve.wait_ge(stored[slot], 16 * (q - 1) + 1)
                    dve.wait_ge(rstd_ok[3], g + 1)
                    apply_norm(3, x4[slot], x4_ok)

            dve.memset(ones[:], 1.0).then_inc(consts_ready, 1)
            dve.memset(zero2[:], 0.0).then_inc(consts_ready, 1)
            dve.memset(eps2[:], LN_EPS).then_inc(consts_ready, 1)
            dve.memset(minus_half2[:], -0.5).then_inc(consts_ready, 1)
            for k in range(RING):
                dve.memset(x4[k][:], 0.0).then_inc(stored[k], 1)
            dve.wait_ge(consts_ready, 5)
            dve.tensor_copy(ones_r[:], ones[:]).then_inc(consts_ready, 1)
            for rt in range(NT):
                dve.tensor_copy(y[0][:, rt, F:F + 2], ones[:]).then_inc(consts_ready, 1)
            dve.wait_ge(w_in["w0"], 32)
            for ct in range(NT):
                if ct:
                    dve.wait_ge(wa_ready, ct)
                dve.tensor_tensor_reduce(junk[:], w0_raw[:, ct, 0:F], a_rows[:], 1.0, 0.0, ALU.mult, ALU.add,
                                         wa_col[:, ct:ct + 1]).then_inc(wa_ready, 1)
            dve.wait_ge(wa_ready, NT)
            for c in range(2):
                ins = dve.tensor_copy(w0_raw[:, :, F + c:F + c + 1], wa_col[:].rearrange("p (t c) -> p t c", c=1))
            ins.then_inc(w0_widened, 1)

            def rest_w1_w2():
                dve.wait_ge(w_hi["w1"], 1)
                rest(W1[1][:], raws["w1"][:], W1[0][:], w_lo["w1"])
                dve.wait_ge(w_hi["w2"], 1)
                rest(W2[1][:], raws["w2"][:], W2[0][:], w_lo["w2"])

            def rest_others():
                dve.wait_ge(w_hi["w3"], 1)
                rest(W3[1][:], raws["w3"][:], W3[0][:], w_lo["w3"])
                dve.wait_ge(w_hi["wg"], 1)
                rest(WG[1][:], raws["wg"][:], WG[0][:], w_lo["wg"])
                dve.wait_ge(w_hi["wc"], 1)
                rest(WS[1][:], psD[:], WS[0][:], w_lo["wc"])
                dve.wait_ge(w_hi["wc"], 2)
                rest(WN[1][:], psU[:], WN[0][:], w_lo["wc"])

            dve.wait_ge(w_hi["w0"], 1)
            rest(W0[1][:], w0_raw[:], W0[0][:], w_lo["w0"])
            steps(dve, step, {1: rest_w1_w2, 2: rest_others})

        @block.gpsimd
        def _(pool):
            def rest(dst, full, hi, done):
                pool.tensor_tensor(dst, full, hi.bitcast(F32), ALU.subtract).then_inc(done, 1)

            def step(t, q, k):
                if live(t - 2):
                    g, slot = t - 2, (k - 2) % RING
                    pool.wait_ge(x1_ok, g + 1)
                    if live(g - 2):
                        pool.wait_ge(res_ok[1], g - 1)
                    if first(g):
                        pool.wait_ge(biases_loaded, 16 * N_BIASES)
                    pool.tensor_tensor(x1_b3[slot % 2][:], x1[:], b3_rows[:], ALU.add).then_inc(x1_b3_ok, 1)
                if live(t - 3):
                    g, slot = t - 3, (k - 3) % RING
                    pool.wait_ge(deg_ok, g + 1)
                    pool.tensor_tensor(dinv[slot % 2][:], deg[:], minus_half2[:], ALU.pow).then_inc(dinv_ok, 1)
                if live(t - 1):
                    g, slot = t - 1, (k - 1) % RING
                    pool.wait_ge(adj_hi, g + 1)
                    rest(adjT[slot][1][:], adjT_full[slot % 2][:], adjT[slot][0][:], adj_lo)
                if live(t - 2):
                    g, slot = t - 2, (k - 2) % RING
                    pool.wait_ge(h2_hi, g + 1)
                    rest(h2T[1][:], h2T_full[:], h2T[0][:], h2_lo)
                if live(t - 3):
                    g, slot = t - 3, (k - 3) % RING
                    pool.wait_ge(agg_tanh, g + 1)
                    if live(g - 1):
                        pool.wait_ge(x3_ok, g)
                    pool.tensor_tensor(res[2][:], agg[:], x2[slot % 2][:], ALU.add).then_inc(res_ok[2], 1)
                    pool.wait_ge(mean_var_ok[2], g + 1)
                    pool.tensor_tensor(var_eps[2][:], mean_var[2][:, :, 1], eps2[:], ALU.add)
                    pool.tensor_tensor(neg_mean[2][:], zero2[:], mean_var[2][:, :, 0], ALU.subtract).then_inc(var_ok[2], 1)
                    pool.wait_ge(var_ok[2], g + 1)
                    if live(g - 1):
                        pool.wait_ge(x3_ok, g)
                    pool.tensor_tensor(rstd[2][:], var_eps[2][:], minus_half2[:], ALU.pow).then_inc(rstd_ok[2], 1)
                    pool.wait_ge(rstd_ok[2], g + 1)
                    pool.tensor_tensor(shift[2][:], neg_mean[2][:], rstd[2][:], ALU.mult).then_inc(shift_ok[2], 1)
                if live(t - 4):
                    g, slot = t - 4, (k - 4) % RING
                    pool.wait_ge(relu_ok, g + 1)
                    pool.tensor_tensor(res[3][:], pre_relu[:], x3[slot % 2][:], ALU.add).then_inc(res_ok[3], 1)
                if live(t - 1):
                    g, slot = t - 1, (k - 1) % RING
                    pool.wait_ge(h1_hi, g + 1)
                    rest(h1T[1][:], h1T_full[:], h1T[0][:], h1_lo)
                if live(t - 2):
                    g, slot = t - 2, (k - 2) % RING
                    pool.wait_ge(mean_var_ok[1], g + 1)
                    pool.tensor_tensor(var_eps[1][:], mean_var[1][:, :, 1], eps2[:], ALU.add)
                    pool.tensor_tensor(neg_mean[1][:], zero2[:], mean_var[1][:, :, 0], ALU.subtract).then_inc(var_ok[1], 1)
                    pool.wait_ge(var_ok[1], g + 1)
                    if live(g - 1):
                        pool.wait_ge(x2_ok, g)
                    pool.tensor_tensor(rstd[1][:], var_eps[1][:], minus_half2[:], ALU.pow).then_inc(rstd_ok[1], 1)
                    pool.wait_ge(rstd_ok[1], g + 1)
                    pool.tensor_tensor(shift[1][:], neg_mean[1][:], rstd[1][:], ALU.mult).then_inc(shift_ok[1], 1)
                if live(t - 4):
                    g, slot = t - 4, (k - 4) % RING
                    pool.wait_ge(mean_var_ok[3], g + 1)
                    pool.tensor_tensor(var_eps[3][:], mean_var[3][:, :, 1], eps2[:], ALU.add).then_inc(var_ok[3], 1)
                    pool.wait_ge(var_ok[3], g + 1)
                    pool.tensor_tensor(rstd[3][:], var_eps[3][:], minus_half2[:], ALU.pow).then_inc(rstd_ok[3], 1)
                if live(t):
                    g, slot = t, k
                    pool.wait_ge(mean_var_ok[0], g + 1)
                    pool.tensor_tensor(var_eps[0][:], mean_var[0][:, :, 1], eps2[:], ALU.add).then_inc(var_ok[0], 1)
                    pool.wait_ge(var_ok[0], g + 1)
                    if live(g - 1):
                        pool.wait_ge(x1_ok, g)
                    pool.tensor_tensor(rstd[0][:], var_eps[0][:], minus_half2[:], ALU.pow).then_inc(rstd_ok[0], 1)

            pool.memset(eye[:], 0.0).then_inc(eye_cleared, 1)
            pool.wait_ge(eye_cleared, 1)
            pool.affine_select(out=eye[:], in_=eye[:], compare_op=ALU.not_equal, fill=1.0, base=0,
                               pattern=[[P, NT], [-1, N]], channel_multiplier=1).then_inc(consts_ready, 1)
            pool.wait_ge(consts_ready, N_CONSTS)
            steps(pool, step)


_INS = ['x', 'adj', 'L0_gnn_w', 'L0_gnn_a', 'L1_gnn_W1', 'L1_gnn_b1', 'L1_gnn_W2', 'L1_gnn_b2', 'L1_gnn_W3',
        'L1_gnn_b3', 'L2_gnn_W', 'L2_gnn_b', 'L3_gnn_W']


def kernel(**inputs):
    import numpy as _np
    import concourse.bacc as _bacc
    from concourse import mybir as _mybir
    from concourse.bass_utils import run_bass_kernel_spmd as _run

    nc = _bacc.Bacc("TRN2", target_bir_lowering=False, num_devices=1)
    arrays, args = {}, []
    for name in _INS:
        a = _np.ascontiguousarray(inputs[name])
        arrays[f"in_{name}_dram"] = a
        args.append(nc.dram_tensor(f"in_{name}_dram", a.shape, _mybir.dt.from_np(a.dtype), kind="ExternalInput").ap())
    args.append(nc.dram_tensor("out_0_dram", inputs['x'].shape, _mybir.dt.float32, kind="ExternalOutput").ap())
    resnorm_gnn_stack(nc, *args)
    r = _run(nc, [arrays], core_ids=[0])
    return r.results[0]["out_0_dram"]
```

```python
from contextlib import ExitStack

import concourse.bass as bass
from concourse import mybir

P = 128
F32 = mybir.dt.float32
F32R = mybir.dt.float32r
ALU = mybir.AluOpType
ACT = mybir.ActivationFunctionType

LN_EPS = 1e-5
DEG_EPS = 1e-6
RING = 4


def resnorm_gnn_stack(nc, x, adj, w0, a0, w1, b1, w2, b2, w3, b3, wg, bg, wc, out):
    G, N, F = x.shape
    NT = N // P
    assert NT == 2 and F == N
    QUADS = G // RING

    with ExitStack() as ctx:
        def sb(name, shape, dt=F32):
            return ctx.enter_context(nc.sbuf_tensor(name, [P, *shape], dt))

        def split(name, width=F):
            return sb(name + "_hi", [NT, width], F32R), sb(name + "_lo", [NT, width], F32R)

        def sem(name):
            return ctx.enter_context(nc.semaphore(name))

        eye = sb("eye", [NT, N])
        ident = eye[:, 0, 0:P]
        zero2 = sb("zero2", [NT])
        eps2 = sb("eps2", [NT])
        minus_half2 = sb("minus_half2", [NT])
        wait_pad = [sb(f"wait_pad{n}", [1]) for n in range(4)]
        raws = {n: sb(n + "_raw", [NT, F]) for n in ("w0", "w1", "w2", "w3", "wg")}
        wc_raw = sb("wc_raw", [NT, 2 * F])
        wa_terms = sb("wa_terms", [NT, F])
        still = sb("still", [F], F32R)
        a_rows = sb("a_rows", [F])
        wa_col = sb("wa_col", [NT])
        wa_rows = sb("wa_rows", [F])
        b3_rows = sb("b3_rows", [NT, F])
        bg_rows = sb("bg_rows", [NT, F])
        b1_col = sb("b1_col", [NT])
        b2_col = sb("b2_col", [NT])
        W0, W1, W2, W3, WG = split("w0"), split("w1"), split("w2"), split("w3"), split("wg")
        WS, WN = split("w_self"), split("w_neigh")

        x_in = [sb(f"x_in{k}", [NT, F]) for k in range(RING)]
        adj_in = [sb(f"adj_in{k}", [NT, N]) for k in range(RING)]
        adjT = [split(f"adjT{k}", N) for k in range(RING)]
        linkT = [sb(f"linkT{k}", [NT, N], F32R) for k in range(RING)]
        rowsum = [sb(f"rowsum{k}", [NT]) for k in range(RING)]
        inv_deg = [sb(f"inv_deg{k}", [NT]) for k in range(RING)]
        esum = [sb(f"esum{k}", [NT]) for k in range(RING)]
        inv_esum = [sb(f"inv_esum{k}", [NT]) for k in range(RING)]
        ratio = [sb(f"ratio{k}", [NT]) for k in range(RING)]
        deg_floor = [sb(f"deg_floor{k}", [NT]) for k in range(RING)]
        links = [sb(f"links{k}", [NT]) for k in range(RING)]
        dinv = [sb(f"dinv{k}", [NT]) for k in range(RING)]
        adjT_full = [sb(f"adjT_full{k}", [NT, N]) for k in range(2)]
        x0 = split("x0")
        s_col = sb("s_col", [NT])
        gate = sb("gate", [NT, N])
        gate_leaky = sb("gate_leaky", [NT, N])
        s_terms = sb("s_terms", [NT, F])
        esum_terms = sb("esum_terms", [NT, N])
        link_terms = sb("link_terms", [NT, N])
        adj_copy = sb("adj_copy", [NT, N])
        eT_full = sb("eT_full", [NT, N])
        eT = split("eT", N)
        ExT = split("ExT", N)
        x1_parts, a1T = split("x1_parts"), split("a1T", N)
        sup2, sup3 = split("sup2"), split("sup3")
        h1T_full, h2T_full = sb("h1T_full", [NT, N]), sb("h2T_full", [NT, N])
        h1T, h2T = split("h1T", N), split("h2T", N)
        msg, a2T = split("msg"), split("a2T", N)
        agg = sb("agg", [NT, F])
        x3T, z = split("x3T", N), split("z")
        u_self = sb("u_self", [NT, F])
        pre_relu = sb("pre_relu", [NT, F])
        res = [sb(f"res{n}", [NT, F]) for n in range(4)]
        x1 = sb("x1", [NT, F])
        x1_b3 = [sb(f"x1_b3_{k}", [NT, F]) for k in range(2)]
        x2 = [sb(f"x2_{k}", [NT, F]) for k in range(2)]
        x3 = [sb(f"x3_{k}", [NT, F]) for k in range(2)]
        x4 = [sb(f"x4_{k}", [NT, F]) for k in range(RING)]
        stats = [sb(f"stats{n}", [NT, 6]) for n in range(4)]
        mean_var = [sb(f"mean_var{n}", [NT, 2]) for n in range(4)]
        var_eps = [sb(f"var_eps{n}", [NT]) for n in range(4)]
        neg_mean = [sb(f"neg_mean{n}", [NT]) for n in range(4)]
        rstd = [sb(f"rstd{n}", [NT]) for n in range(4)]
        shift = [sb(f"shift{n}", [NT]) for n in range(4)]

        ps_s, ps_adj, ps_ex, ps_l0, ps_l1, ps_l1b, ps_l2, ps_u = (
            ctx.enter_context(nc.psum_tensor(n, [P, NT, F], F32))
            for n in ("ps_s", "ps_adj", "ps_ex", "ps_l0", "ps_l1", "ps_l1b", "ps_l2", "ps_u"))
        s_bcast = ps_s[:, 0, :]

        x_loaded = [sem(f"x_loaded{k}") for k in range(RING)]
        adj_loaded = [sem(f"adj_loaded{k}") for k in range(RING)]
        stored = [sem(f"stored{k}") for k in range(RING)]
        WEIGHTS = ("w0", "w1", "w2", "w3", "wg", "wc")
        w_in = {n: sem(n + "_loaded") for n in WEIGHTS}
        w_hi = {n: sem(n + "_hi_ready") for n in WEIGHTS}
        w_lo = {n: sem(n + "_lo_ready") for n in WEIGHTS}
        biases_loaded, consts_ready, wa_turned, wa_copied, wc_turned, wa_ready, eye_cleared, still_ready = (
            sem(n) for n in ("biases_loaded", "consts_ready", "wa_turned", "wa_copied", "wc_turned",
                             "wa_ready", "eye_cleared", "still_ready"))
        (adjT_mm, s_mm, ExT_mm, l0_mm, a1T_mm, h1_mm, sup2_mm, h2_mm, sup3_mm, o3_mm, a2T_mm, agg_mm, x3T_mm,
         z_mm, u_mm, v_mm) = (
            sem(n) for n in ("adjT_mm", "s_mm", "ExT_mm", "l0_mm", "a1T_mm", "h1_mm", "sup2_mm", "h2_mm",
                "sup3_mm", "o3_mm", "a2T_mm", "agg_mm", "x3T_mm", "z_mm", "u_mm", "v_mm"))
        (adjT_ok, rowsum_ok, gate_tanh, gate_ok, x1_ok, x2_ok, x3_ok, x4_ok, ExT_hi, a1T_hi, h1_full, sup2_hi,
         h2_full, sup3_hi, a2T_hi, msg_hi, agg_tanh, x3T_hi, z_hi, u_ok, x1_hi, adj_hi, e_hi, h1_hi, h2_hi) = (
            sem(n) for n in ("adjT_ok", "rowsum_ok", "gate_tanh", "gate_ok", "x1_ok", "x2_ok", "x3_ok", "x4_ok",
                "ExT_hi", "a1T_hi", "h1_full", "sup2_hi", "h2_full", "sup3_hi", "a2T_hi", "msg_hi", "agg_tanh",
                "x3T_hi", "z_hi", "u_ok", "x1_hi", "adj_hi", "e_hi", "h1_hi", "h2_hi"))
        (x0_hi, x1_lo, s_ok, esum_ok, ratio_ok, inv_esum_ok, floor_ok, links_ok, link_ok, gate_leaky_ok, e_full,
         ExT_lo, a1T_lo, sup2_lo, sup3_lo, a2T_lo, msg_lo, agg_scaled, x3T_lo, z_lo, inv_deg_ok, v_ok) = (
            sem(n) for n in ("x0_hi", "x1_lo", "s_ok", "esum_ok", "ratio_ok", "inv_esum_ok", "floor_ok",
                "links_ok", "link_ok", "gate_leaky_ok", "e_full", "ExT_lo", "a1T_lo", "sup2_lo", "sup3_lo",
                "a2T_lo", "msg_lo", "agg_scaled", "x3T_lo", "z_lo", "inv_deg_ok", "v_ok"))
        (x0_lo, e_lo, h1_lo, h2_lo, adj_lo, dinv_ok, x1_b3_ok) = (
            sem(n) for n in ("x0_lo", "e_lo", "h1_lo", "h2_lo", "adj_lo", "dinv_ok", "x1_b3_ok"))

        res_ok = [sem(f"res_ok{n}") for n in range(4)]
        stats_ok = [sem(f"stats_ok{n}") for n in range(4)]
        mean_var_ok = [sem(f"mean_var_ok{n}") for n in range(4)]
        var_ok = [sem(f"var_ok{n}") for n in range(4)]
        rstd_ok = [sem(f"rstd_ok{n}") for n in range(4)]
        shift_ok = [sem(f"shift_ok{n}") for n in range(4)]

        N_BIASES = 2 + 2 * NT
        N_CONSTS = 4
        block = ctx.enter_context(nc.Block())

        def steps(eng, step):
            for k in range(RING):
                step(k, 0, k)
            with eng.Fori(1, QUADS) as q:
                for k in range(RING):
                    step(q * RING + k, q, k)
            for k in range(RING):
                step(G + k, QUADS, k)

        def live(g):
            return not isinstance(g, int) or 0 <= g < G

        def first(g):
            return isinstance(g, int) and g == 0

        def last(g):
            return isinstance(g, int) and g == G - 1

        @block.sync
        def _(sp):
            def load(q, k):
                sp.dma_start(x_in[k][:], x_q[q, k]).then_inc(x_loaded[k], 16)
                sp.dma_start(adj_in[k][:], adj_q[q, k]).then_inc(adj_loaded[k], 16)

            x_q = x.rearrange("(q k) (t p) f -> q k p t f", k=RING, p=P)
            adj_q = adj.rearrange("(q k) (t p) f -> q k p t f", k=RING, p=P)

            out_q = out.rearrange("(q k) (t p) f -> q k p t f", k=RING, p=P)

            def rows(v):
                return v.rearrange("(a f) -> a f", a=1).broadcast_to([P, F])

            def cols(v):
                return v.rearrange("(t p) -> p t", p=P)

            def weight(n, dst, src):
                sp.dma_start(dst, src.rearrange("(t p) h -> p t h", p=P)).then_inc(w_in[n], 16)

            weight("w0", raws["w0"][:], w0)
            sp.dma_start(a_rows[:], rows(a0)).then_inc(w_in["w0"], 16)
            load(0, 0)
            weight("w1", raws["w1"][:], w1)
            weight("wc", wc_raw[:], wc)
            sp.dma_start(x_in[1][:], x_q[0, 1]).then_inc(x_loaded[1], 16)
            weight("w2", raws["w2"][:], w2)
            sp.dma_start(adj_in[1][:], adj_q[0, 1]).then_inc(adj_loaded[1], 16)
            weight("w3", raws["w3"][:], w3)
            weight("wg", raws["wg"][:], wg)
            load(0, 2)
            with nc.allow_non_contiguous_dma(reason="two short columns, once"):
                sp.dma_start(b1_col[:], cols(b1)).then_inc(biases_loaded, 16)
                sp.dma_start(b2_col[:], cols(b2)).then_inc(biases_loaded, 16)
            for t in range(NT):
                sp.dma_start(b3_rows[:, t, :], rows(b3)).then_inc(biases_loaded, 16)
                sp.dma_start(bg_rows[:, t, :], rows(bg)).then_inc(biases_loaded, 16)
            load(0, 3)

            def reload(q, k):
                g = q * RING + k - RING
                sp.wait_ge(adjT_mm, g + 1)
                sp.wait_ge(rowsum_ok, g + 1)
                sp.wait_ge(links_ok, g + 1)
                sp.wait_ge(res_ok[0], g + 1)
                load(q, k)

            def store(q, k):
                sp.wait_ge(x4_ok, q * RING + k + 1)
                sp.dma_start(out_q[q, k], x4[k][:]).then_inc(stored[k], 16)

            for k in range(RING):
                reload(1, k)
            with sp.Fori(2, QUADS) as q:
                for k in range(RING):
                    reload(q, k)
                    store(q - 2, k)
            for q in (QUADS - 2, QUADS - 1):
                for k in range(RING):
                    store(q, k)
            for k in range(RING):
                sp.wait_ge(stored[k], 16 * QUADS + 1)

        @block.tensor
        def _(pe):
            def turn(dst, src, done):
                for rt in range(NT):
                    for ct in range(NT):
                        mm = pe.transpose(dst[:, ct, rt * P:(rt + 1) * P], src[:, rt, ct * P:(ct + 1) * P], ident)
                mm.then_inc(done, 1)

            def keep_warm(bank, n):
                for _ in range(n):
                    pe.matmul(bank[:, 0, :], still[:, 0:P], still[:], start=True, stop=True,
                              skip_group_check=True)

            def product(dst, left, right, done):
                passes = [(l, r) for l in range(len(left)) for r in range(len(right)) if l + r < 2]
                for rt in range(NT):
                    n = 0
                    for ct in range(NT):
                        for l, r in passes:
                            mm = pe.matmul(dst[:, rt, :], left[l][:, ct, rt * P:(rt + 1) * P],
                                           right[r][:, ct, :], start=(n == 0), stop=(n == NT * len(passes) - 1),
                                           skip_group_check=True)
                            n += 1
                mm.then_inc(done, 1)

            def turn_wc():
                pe.wait_ge(w_in["wc"], 16)
                turn(ps_l2, wc_raw[:, :, 0:F], wc_turned)
                turn(ps_u, wc_raw[:, :, F:2 * F], wc_turned)

            def spread(dst, col, done):
                for rt in range(NT):
                    mm = pe.transpose(dst[:, rt * P:(rt + 1) * P], col[:, rt:rt + 1].broadcast_to([P, P]), ident)
                mm.then_inc(done, 1)

            def step(t, q, k):
                if live(t - 3):
                    g, slot = t - 3, (k - 3) % RING
                    pe.wait_ge(h2_hi, g + 1)
                    pe.wait_ge(h2_lo, g + 1)
                    if first(g):
                        pe.wait_ge(w_lo["w3"], 1)
                    product(ps_l1b, h2T, W3, sup3_mm)
                if live(t - 2):
                    g, slot = t - 2, (k - 2) % RING
                    pe.wait_ge(a1T_lo, g + 1)
                    if first(g):
                        pe.wait_ge(w_lo["w1"], 1)
                    product(ps_l1, W1, a1T, h1_mm)
                if live(t - 1):
                    g, slot = t - 1, (k - 1) % RING
                    if first(g):
                        turn_wc()
                        keep_warm(ps_l1b, 5)
                    pe.wait_ge(e_hi, g + 1)
                    pe.wait_ge(e_lo, g + 1)
                    pe.wait_ge(x0_lo, g + 1)
                    if live(g - 1):
                        pe.wait_ge(ExT_lo, g)
                    product(ps_ex, x0, eT, ExT_mm)
                if live(t - 3):
                    g, slot = t - 3, (k - 3) % RING
                    if last(g):
                        pe.wait_ge(adjT_ok, G)
                        keep_warm(ps_adj, 14)
                    pe.wait_ge(sup3_lo, g + 1)
                    product(ps_l1b, adjT[slot], sup3, o3_mm)
                if live(t):
                    g, slot = t, k
                    pe.wait_ge(s_ok, g + 1)
                    if live(g - 1):
                        pe.wait_ge(gate_tanh, g)
                    spread(s_bcast, s_col, s_mm)
                if live(t - 1):
                    g, slot = t - 1, (k - 1) % RING
                    pe.wait_ge(ExT_lo, g + 1)
                    if live(g - 1):
                        pe.wait_ge(res_ok[0], g)
                    if first(g):
                        pe.wait_ge(w_lo["w0"], 1)
                    product(ps_l0, ExT, W0, l0_mm)
                if live(t - 4):
                    g, slot = t - 4, (k - 4) % RING
                    if isinstance(g, int) and g == G - 3:
                        pe.wait_ge(adjT_ok, G)
                        keep_warm(ps_adj, 19)
                    if isinstance(g, int) and g == G - 2:
                        pe.wait_ge(adjT_ok, G)
                        keep_warm(ps_adj, 10)
                    if last(g):
                        pe.wait_ge(adjT_ok, G)
                        keep_warm(ps_adj, 30)
                    pe.wait_ge(x3_ok, g + 1)
                    turn(ps_l2, x3[slot % 2], x3T_mm)
                if live(t):
                    g, slot = t, k
                    pe.wait_ge(adj_loaded[slot], 16 * q + 16)
                    if live(g - 1):
                        pe.wait_ge(adjT_ok, g)
                    turn(ps_adj, adj_in[slot], adjT_mm)
                if live(t - 2):
                    g, slot = t - 2, (k - 2) % RING
                    pe.wait_ge(h1_hi, g + 1)
                    pe.wait_ge(h1_lo, g + 1)
                    if live(g - 1):
                        pe.wait_ge(res_ok[1], g)
                    if first(g):
                        pe.wait_ge(w_lo["w2"], 1)
                    product(ps_l1b, h1T, W2, sup2_mm)
                if live(t - 4):
                    g, slot = t - 4, (k - 4) % RING
                    if isinstance(g, int) and g == G - 2:
                        pe.wait_ge(adjT_ok, G)
                        keep_warm(ps_adj, 7)
                    if last(g):
                        pe.wait_ge(adjT_ok, G)
                        keep_warm(ps_adj, 7)
                    pe.wait_ge(x3T_lo, g + 1)
                    if first(g):
                        pe.wait_ge(w_lo["wc"], 2)
                    product(ps_l2, x3T, WN, z_mm)
                    pe.wait_ge(x3T_lo, g + 1)
                    if live(g - 1):
                        pe.wait_ge(v_ok, g)
                    if first(g):
                        pe.wait_ge(w_lo["wc"], 2)
                    product(ps_u, x3T, WS, u_mm)
                if live(t - 2):
                    g, slot = t - 2, (k - 2) % RING
                    pe.wait_ge(sup2_lo, g + 1)
                    product(ps_l1b, sup2, adjT[slot], h2_mm)
                if live(t - 3):
                    g, slot = t - 3, (k - 3) % RING
                    pe.wait_ge(msg_lo, g + 1)
                    pe.wait_ge(link_ok, g + 1)
                    if live(g - 1):
                        pe.wait_ge(z_lo, g)
                    product(ps_l2, msg, (linkT[slot],), a2T_mm)
                if live(t - 4):
                    g, slot = t - 4, (k - 4) % RING
                    if last(g):
                        pe.wait_ge(adjT_ok, G)
                        keep_warm(ps_adj, 7)
                    pe.wait_ge(z_lo, g + 1)
                    pe.wait_ge(u_ok, g + 1)
                    product(ps_u, adjT[slot], z, v_mm)
                if live(t - 1):
                    g, slot = t - 1, (k - 1) % RING
                    if first(g):
                        keep_warm(ps_l1b, 24)
                    pe.wait_ge(x1_hi, g + 1)
                    pe.wait_ge(x1_lo, g + 1)
                    pe.wait_ge(adj_hi, g + 1)
                    pe.wait_ge(adj_lo, g + 1)
                    if live(g - 1):
                        pe.wait_ge(h1_full, g)
                    product(ps_l1, x1_parts, adjT[slot], a1T_mm)
                if live(t - 3):
                    g, slot = t - 3, (k - 3) % RING
                    pe.wait_ge(a2T_lo, g + 1)
                    if first(g):
                        pe.wait_ge(w_lo["wg"], 1)
                    product(ps_l2, a2T, WG, agg_mm)

            pe.wait_ge(still_ready, 1)
            keep_warm(ps_l1b, 15)
            pe.wait_ge(consts_ready, N_CONSTS)
            pe.wait_ge(wa_ready, NT)
            spread(s_bcast, wa_col, wa_turned)
            steps(pe, step)

        @block.scalar
        def _(act):
            def copy(dst, src, done):
                act.activation(dst, src, ACT.Identity).then_inc(done, 1)

            def apply_norm(n, dst, done):
                for rt in range(NT):
                    ins = act.activation(dst[:, rt, :], res[n][:, rt, :], ACT.Identity, bias=shift[n][:, rt:rt + 1],
                                         scale=rstd[n][:, rt:rt + 1])
                ins.then_inc(done, 1)

            def round_w1_w2_wc():
                act.wait_ge(w_in["w1"], 16)
                copy(W1[0][:], raws["w1"][:], w_hi["w1"])
                act.wait_ge(w_in["w2"], 16)
                copy(W2[0][:], raws["w2"][:], w_hi["w2"])
                act.wait_ge(wc_turned, 2)
                copy(WS[0][:], ps_l2[:], w_hi["wc"])
                copy(WN[0][:], ps_u[:], w_hi["wc"])

            def round_w3_wg():
                act.wait_ge(w_in["w3"], 16)
                copy(W3[0][:], raws["w3"][:], w_hi["w3"])
                act.wait_ge(w_in["wg"], 16)
                copy(WG[0][:], raws["wg"][:], w_hi["wg"])

            def step(t, q, k):
                if live(t):
                    g, slot = t, k
                    act.wait_ge(s_mm, g + 1)
                    if live(g - 1):
                        act.wait_ge(e_full, g)
                        act.wait_ge(esum_ok, g)
                    for rt in range(NT):
                        ins = act.activation(gate[:, rt, :], s_bcast, ACT.Tanh, bias=s_col[:, rt:rt + 1])
                    ins.then_inc(gate_tanh, 1)
                if live(t - 4):
                    g, slot = t - 4, (k - 4) % RING
                    act.wait_ge(x3T_mm, g + 1)
                    copy(x3T[0][:], ps_l2[:], x3T_hi)
                if live(t):
                    g, slot = t, k
                    if isinstance(g, int) and g == 1:
                        round_w3_wg()
                    act.wait_ge(adjT_mm, g + 1)
                    if live(g - 2):
                        act.wait_ge(adj_lo, g - 1)
                        act.wait_ge(e_full, g - 1)
                        act.wait_ge(link_ok, g - 1)
                    copy(adjT_full[slot % 2][:], ps_adj[:], adjT_ok)
                if live(t - 3):
                    g, slot = t - 3, (k - 3) % RING
                    act.wait_ge(shift_ok[1], g + 1)
                    apply_norm(1, x2[slot % 2], x2_ok)
                if live(t - 2):
                    g, slot = t - 2, (k - 2) % RING
                    act.wait_ge(sup2_mm, g + 1)
                    if live(g - 1):
                        act.wait_ge(h2_mm, g)
                    copy(sup2[0][:], ps_l1b[:], sup2_hi)
                if live(t - 3):
                    g, slot = t - 3, (k - 3) % RING
                    act.wait_ge(x2_ok, g + 1)
                    act.wait_ge(dinv_ok, g + 1)
                    if live(g - 1):
                        act.wait_ge(a2T_mm, g)
                    for rt in range(NT):
                        ins = act.activation(msg[0][:, rt, :], x2[slot % 2][:, rt, :], ACT.Identity,
                                             scale=dinv[slot][:, rt:rt + 1])
                    ins.then_inc(msg_hi, 1)
                if live(t - 4):
                    g, slot = t - 4, (k - 4) % RING
                    act.wait_ge(z_mm, g + 1)
                    copy(z[0][:], ps_l2[:], z_hi)
                if live(t):
                    g, slot = t, k
                    act.wait_ge(gate_leaky_ok, g + 1)
                    act.activation(gate[:], gate_leaky[:], ACT.Exp, scale=8.0).then_inc(gate_ok, 1)
                if live(t - 1):
                    g, slot = t - 1, (k - 1) % RING
                    act.wait_ge(shift_ok[0], g + 1)
                    if live(g - 1):
                        act.wait_ge(x1_lo, g)
                        act.wait_ge(x1_b3_ok, g)
                    apply_norm(0, x1, x1_ok)
                if live(t - 4):
                    g, slot = t - 4, (k - 4) % RING
                    act.wait_ge(u_mm, g + 1)
                    copy(u_self[:], ps_u[:], u_ok)
                if live(t - 1):
                    g, slot = t - 1, (k - 1) % RING
                    act.wait_ge(x1_ok, g + 1)
                    if live(g - 1):
                        act.wait_ge(a1T_mm, g)
                    copy(x1_parts[0][:], x1[:], x1_hi)
                if live(t - 2):
                    g, slot = t - 2, (k - 2) % RING
                    act.wait_ge(h2_mm, g + 1)
                    if live(g - 1):
                        act.wait_ge(h2_lo, g)
                    if first(g):
                        act.wait_ge(biases_loaded, 16 * N_BIASES)
                    for ht in range(NT):
                        ins = act.activation(h2T_full[:, ht, :], ps_l1b[:, ht, :], ACT.Relu,
                                             bias=b2_col[:, ht:ht + 1])
                    ins.then_inc(h2_full, 1)
                if live(t - 3):
                    g, slot = t - 3, (k - 3) % RING
                    act.wait_ge(a2T_mm, g + 1)
                    if live(g - 1):
                        act.wait_ge(agg_mm, g)
                    copy(a2T[0][:], ps_l2[:], a2T_hi)
                if live(t - 2):
                    g, slot = t - 2, (k - 2) % RING
                    act.wait_ge(h2_full, g + 1)
                    if live(g - 1):
                        act.wait_ge(sup3_mm, g)
                    copy(h2T[0][:], h2T_full[:], h2_hi)
                if live(t):
                    g, slot = t, k
                    act.wait_ge(adj_loaded[slot], 16 * q + 16)
                    if live(g - 4):
                        act.wait_ge(floor_ok, g - 3)
                        act.wait_ge(ratio_ok, g - 3)
                    for rt in range(NT):
                        ins = act.activation(adj_copy[:, rt, :], adj_in[slot][:, rt, :], ACT.Identity,
                                             accum_out=rowsum[slot][:, rt:rt + 1])
                    ins.then_inc(rowsum_ok, 1)
                if live(t - 1):
                    g, slot = t - 1, (k - 1) % RING
                    act.wait_ge(a1T_mm, g + 1)
                    if live(g - 1):
                        act.wait_ge(h1_mm, g)
                    copy(a1T[0][:], ps_l1[:], a1T_hi)
                if live(t):
                    g, slot = t, k
                    act.wait_ge(e_full, g + 1)
                    if live(g - 1):
                        act.wait_ge(ExT_mm, g)
                    copy(eT[0][:], eT_full[:], e_hi)
                    act.wait_ge(adjT_ok, g + 1)
                    if live(g - 4):
                        act.wait_ge(v_mm, g - 3)
                    copy(adjT[slot][0][:], adjT_full[slot % 2][:], adj_hi)
                if live(t - 3):
                    g, slot = t - 3, (k - 3) % RING
                    act.wait_ge(agg_scaled, g + 1)
                    act.activation(agg[:], agg[:], ACT.Tanh).then_inc(agg_tanh, 1)
                if live(t - 2):
                    g, slot = t - 2, (k - 2) % RING
                    act.wait_ge(sup3_mm, g + 1)
                    if live(g - 1):
                        act.wait_ge(o3_mm, g)
                    copy(sup3[0][:], ps_l1b[:], sup3_hi)
                if live(t - 1):
                    g, slot = t - 1, (k - 1) % RING
                    act.wait_ge(h1_mm, g + 1)
                    if live(g - 1):
                        act.wait_ge(h1_lo, g)
                    if first(g):
                        act.wait_ge(biases_loaded, 16 * N_BIASES)
                    for ht in range(NT):
                        ins = act.activation(h1T_full[:, ht, :], ps_l1[:, ht, :], ACT.Relu,
                                             bias=b1_col[:, ht:ht + 1])
                    ins.then_inc(h1_full, 1)
                    act.wait_ge(h1_full, g + 1)
                    if live(g - 1):
                        act.wait_ge(sup2_mm, g)
                    copy(h1T[0][:], h1T_full[:], h1_hi)
                if live(t):
                    g, slot = t, k
                    if first(g):
                        round_w1_w2_wc()
                    act.wait_ge(ExT_mm, g + 1)
                    if live(g - 1):
                        act.wait_ge(l0_mm, g)
                    copy(ExT[0][:], ps_ex[:], ExT_hi)
                if live(t - 4):
                    g, slot = t - 4, (k - 4) % RING
                    act.wait_ge(stored[slot], 16 * (q - 1) + 1)
                    act.wait_ge(shift_ok[3], g + 1)
                    apply_norm(3, x4[slot], x4_ok)
                if live(t - 3):
                    g, slot = t - 3, (k - 3) % RING
                    act.wait_ge(shift_ok[2], g + 1)
                    apply_norm(2, x3[slot % 2], x3_ok)


            act.wait_ge(w_in["w0"], 32)
            copy(W0[0][:], raws["w0"][:], w_hi["w0"])
            steps(act, step)

        @block.vector
        def _(dve):
            def copy(dst, src, done):
                dve.tensor_copy(dst, src).then_inc(done, 1)

            def rest(dst, full, hi, done):
                dve.tensor_tensor(dst, full, hi.bitcast(F32), ALU.subtract).then_inc(done, 1)

            def norm_stats(n, g):
                dve.wait_ge(res_ok[n], g + 1)
                for rt in range(NT):
                    ins = dve.bn_stats(stats[n][:, rt, :], res[n][:, rt, :])
                ins.then_inc(stats_ok[n], 1)

            def norm_mean_var(n):
                dve.memset(wait_pad[n][:], 0.0)
                for rt in range(NT):
                    ins = dve.bn_aggr(mean_var[n][:, rt, :], stats[n][:, rt, :])
                ins.then_inc(mean_var_ok[n], 1)

            def rest_wc():
                dve.wait_ge(w_hi["wc"], 1)
                rest(WS[1][:], ps_l2[:], WS[0][:], w_lo["wc"])
                dve.wait_ge(w_hi["wc"], 2)
                rest(WN[1][:], ps_u[:], WN[0][:], w_lo["wc"])

            def rest_w3_wg():
                dve.wait_ge(w_hi["w3"], 1)
                rest(W3[1][:], raws["w3"][:], W3[0][:], w_lo["w3"])
                dve.wait_ge(w_hi["wg"], 1)
                rest(WG[1][:], raws["wg"][:], WG[0][:], w_lo["wg"])

            def step(t, q, k):
                if live(t - 4):
                    g, slot = t - 4, (k - 4) % RING
                    dve.wait_ge(stats_ok[2], g + 1)
                    norm_mean_var(2)
                if live(t):
                    g, slot = t, k
                    if isinstance(g, int) and g == 1:
                        rest_wc()
                    dve.wait_ge(x_loaded[slot], 16 * q + 16)
                    if live(g - 1):
                        dve.wait_ge(gate_tanh, g)
                        dve.wait_ge(s_mm, g)
                    if first(g):
                        dve.wait_ge(wa_copied, 1)
                    for rt in range(NT):
                        ins = dve.scalar_tensor_tensor(out=s_terms[:, rt, :], in0=x_in[slot][:, rt, :], scalar=0.125,
                                                       in1=wa_rows[:], op0=ALU.mult, op1=ALU.mult,
                                                       accum_out=s_col[:, rt:rt + 1])
                    ins.then_inc(s_ok, 1)
                if live(t - 1):
                    g, slot = t - 1, (k - 1) % RING
                    dve.wait_ge(ExT_hi, g + 1)
                    rest(ExT[1][:], ps_ex[:], ExT[0][:], ExT_lo)
                if live(t - 3):
                    g, slot = t - 3, (k - 3) % RING
                    dve.wait_ge(o3_mm, g + 1)
                    dve.wait_ge(x1_b3_ok, g + 1)
                    if live(g - 1):
                        dve.wait_ge(x2_ok, g)
                    dve.tensor_tensor(res[1][:], ps_l1b[:], x1_b3[slot % 2][:], ALU.add).then_inc(res_ok[1], 1)
                if live(t - 4):
                    g, slot = t - 4, (k - 4) % RING
                    dve.wait_ge(rowsum_ok, g + 1)
                    dve.tensor_scalar(deg_floor[slot][:], rowsum[slot][:], DEG_EPS, None,
                                      ALU.max).then_inc(floor_ok, 1)
                if live(t - 3):
                    g, slot = t - 3, (k - 3) % RING
                    norm_stats(1, g)
                    dve.wait_ge(stats_ok[1], g + 1)
                    if live(g - 1):
                        dve.wait_ge(shift_ok[1], g)
                    norm_mean_var(1)
                if live(t - 1):
                    g, slot = t - 1, (k - 1) % RING
                    dve.wait_ge(inv_esum_ok, g + 1)
                    dve.wait_ge(rowsum_ok, g + 1)
                    dve.tensor_tensor(ratio[slot][:], inv_esum[slot][:], rowsum[slot][:],
                                      ALU.mult).then_inc(ratio_ok, 1)
                    if first(g):
                        rest_w3_wg()
                    dve.wait_ge(l0_mm, g + 1)
                    dve.wait_ge(ratio_ok, g + 1)
                    if live(g - 1):
                        dve.wait_ge(x1_ok, g)
                    for rt in range(NT):
                        ins = dve.scalar_tensor_tensor(
                            out=res[0][:, rt, :], in0=ps_l0[:, rt, :], scalar=ratio[slot][:, rt:rt + 1],
                            in1=x_in[slot][:, rt, :], op0=ALU.mult, op1=ALU.add)
                    ins.then_inc(res_ok[0], 1)
                if live(t - 4):
                    g, slot = t - 4, (k - 4) % RING
                    dve.wait_ge(x3T_hi, g + 1)
                    rest(x3T[1][:], ps_l2[:], x3T[0][:], x3T_lo)
                if live(t - 1):
                    g, slot = t - 1, (k - 1) % RING
                    norm_stats(0, g)
                if live(t - 4):
                    g, slot = t - 4, (k - 4) % RING
                    dve.wait_ge(floor_ok, g + 1)
                    dve.reciprocal(inv_deg[slot][:], deg_floor[slot][:]).then_inc(inv_deg_ok, 1)
                if live(t - 1):
                    g, slot = t - 1, (k - 1) % RING
                    dve.wait_ge(stats_ok[0], g + 1)
                    if live(g - 1):
                        dve.wait_ge(shift_ok[0], g)
                    norm_mean_var(0)
                if live(t):
                    g, slot = t, k
                    dve.wait_ge(gate_tanh, g + 1)
                    if live(g - 1):
                        dve.wait_ge(gate_ok, g)
                    dve.scalar_tensor_tensor(out=gate_leaky[:], in0=gate[:], scalar=0.1, in1=gate[:],
                                             op0=ALU.mult, op1=ALU.max).then_inc(gate_leaky_ok, 1)
                if live(t - 2):
                    g, slot = t - 2, (k - 2) % RING
                    dve.wait_ge(sup2_hi, g + 1)
                    rest(sup2[1][:], ps_l1b[:], sup2[0][:], sup2_lo)
                if live(t):
                    g, slot = t, k
                    dve.wait_ge(x_loaded[slot], 16 * q + 16)
                    if live(g - 1):
                        dve.wait_ge(ExT_mm, g)
                    copy(x0[0][:], x_in[slot][:], x0_hi)
                if live(t - 3):
                    g, slot = t - 3, (k - 3) % RING
                    dve.wait_ge(msg_hi, g + 1)
                    for rt in range(NT):
                        ins = dve.scalar_tensor_tensor(
                            out=msg[1][:, rt, :], in0=x2[slot % 2][:, rt, :], scalar=dinv[slot][:, rt:rt + 1],
                            in1=msg[0][:, rt, :].bitcast(F32), op0=ALU.mult, op1=ALU.subtract)
                    ins.then_inc(msg_lo, 1)
                if live(t - 4):
                    g, slot = t - 4, (k - 4) % RING
                    dve.wait_ge(z_hi, g + 1)
                    rest(z[1][:], ps_l2[:], z[0][:], z_lo)
                if live(t):
                    g, slot = t, k
                    dve.wait_ge(gate_ok, g + 1)
                    dve.wait_ge(adjT_ok, g + 1)
                    if live(g - 1):
                        dve.wait_ge(e_lo, g)
                    dve.tensor_tensor(eT_full[:], gate[:], adjT_full[slot % 2][:], ALU.mult).then_inc(e_full, 1)
                    dve.wait_ge(adj_loaded[slot], 16 * q + 16)
                    if live(g - 4):
                        dve.wait_ge(dinv_ok, g - 3)
                    for rt in range(NT):
                        ins = dve.scalar_tensor_tensor(out=link_terms[:, rt, :], in0=adj_in[slot][:, rt, :],
                                                       scalar=0.0, in1=eye[:, rt, :], op0=ALU.not_equal, op1=ALU.max,
                                                       accum_out=links[slot][:, rt:rt + 1])
                    ins.then_inc(links_ok, 1)
                if live(t - 1):
                    g, slot = t - 1, (k - 1) % RING
                    dve.wait_ge(x1_hi, g + 1)
                    rest(x1_parts[1][:], x1[:], x1_parts[0][:], x1_lo)
                if live(t):
                    g, slot = t, k
                    dve.wait_ge(gate_ok, g + 1)
                    dve.wait_ge(adj_loaded[slot], 16 * q + 16)
                    for rt in range(NT):
                        ins = dve.scalar_tensor_tensor(out=esum_terms[:, rt, :], in0=gate[:, rt, :], scalar=1.0,
                                                       in1=adj_in[slot][:, rt, :], op0=ALU.mult, op1=ALU.mult,
                                                       accum_out=esum[slot][:, rt:rt + 1])
                    ins.then_inc(esum_ok, 1)
                if live(t - 3):
                    g, slot = t - 3, (k - 3) % RING
                    dve.wait_ge(a2T_hi, g + 1)
                    rest(a2T[1][:], ps_l2[:], a2T[0][:], a2T_lo)
                if live(t - 4):
                    g, slot = t - 4, (k - 4) % RING
                    dve.wait_ge(v_mm, g + 1)
                    dve.wait_ge(u_ok, g + 1)
                    dve.wait_ge(inv_deg_ok, g + 1)
                    for rt in range(NT):
                        ins = dve.scalar_tensor_tensor(
                            out=pre_relu[:, rt, :], in0=ps_u[:, rt, :], scalar=inv_deg[slot][:, rt:rt + 1],
                            in1=u_self[:, rt, :], op0=ALU.mult, op1=ALU.add)
                    ins.then_inc(v_ok, 1)
                    dve.wait_ge(v_ok, g + 1)
                    dve.scalar_tensor_tensor(out=res[3][:], in0=pre_relu[:], scalar=0.0, in1=x3[slot % 2][:],
                                             op0=ALU.max, op1=ALU.add).then_inc(res_ok[3], 1)
                if live(t - 1):
                    g, slot = t - 1, (k - 1) % RING
                    dve.wait_ge(a1T_hi, g + 1)
                    rest(a1T[1][:], ps_l1[:], a1T[0][:], a1T_lo)
                if live(t - 3):
                    g, slot = t - 3, (k - 3) % RING
                    dve.wait_ge(agg_mm, g + 1)
                    if live(g - 1):
                        dve.wait_ge(res_ok[2], g)
                    if first(g):
                        dve.wait_ge(biases_loaded, 16 * N_BIASES)
                    for rt in range(NT):
                        ins = dve.scalar_tensor_tensor(
                            out=agg[:, rt, :], in0=ps_l2[:, rt, :], scalar=dinv[slot][:, rt:rt + 1],
                            in1=bg_rows[:, rt, :], op0=ALU.mult, op1=ALU.add)
                    ins.then_inc(agg_scaled, 1)
                if live(t - 4):
                    g, slot = t - 4, (k - 4) % RING
                    norm_stats(3, g)
                if live(t - 1):
                    g, slot = t - 1, (k - 1) % RING
                    dve.wait_ge(adjT_ok, g + 1)
                    dve.scalar_tensor_tensor(out=linkT[slot][:], in0=adjT_full[slot % 2][:], scalar=0.0, in1=eye[:],
                                             op0=ALU.not_equal, op1=ALU.max).then_inc(link_ok, 1)
                if live(t - 2):
                    g, slot = t - 2, (k - 2) % RING
                    dve.wait_ge(sup3_hi, g + 1)
                    rest(sup3[1][:], ps_l1b[:], sup3[0][:], sup3_lo)
                if live(t - 4):
                    g, slot = t - 4, (k - 4) % RING
                    dve.wait_ge(stats_ok[3], g + 1)
                    norm_mean_var(3)
                if live(t):
                    g, slot = t, k
                    dve.wait_ge(esum_ok, g + 1)
                    dve.reciprocal(inv_esum[slot][:], esum[slot][:]).then_inc(inv_esum_ok, 1)
                if live(t - 3):
                    g, slot = t - 3, (k - 3) % RING
                    norm_stats(2, g)

            dve.memset(still[:].bitcast(F32), 0.0).then_inc(still_ready, 1)
            dve.memset(zero2[:], 0.0).then_inc(consts_ready, 1)
            dve.memset(eps2[:], LN_EPS).then_inc(consts_ready, 1)
            dve.memset(minus_half2[:], -0.5).then_inc(consts_ready, 1)
            for k in range(RING):
                dve.memset(x4[k][:], 0.0).then_inc(stored[k], 1)
            dve.wait_ge(w_in["w0"], 32)
            for ct in range(NT):
                dve.scalar_tensor_tensor(out=wa_terms[:, ct, :], in0=raws["w0"][:, ct, :], scalar=1.0, in1=a_rows[:],
                                         op0=ALU.mult, op1=ALU.mult,
                                         accum_out=wa_col[:, ct:ct + 1]).then_inc(wa_ready, 1)
            dve.wait_ge(wa_turned, 1)
            dve.tensor_copy(wa_rows[:], s_bcast).then_inc(wa_copied, 1)
            dve.wait_ge(consts_ready, N_CONSTS)
            steps(dve, step)

        @block.gpsimd
        def _(pool):
            def rest(dst, full, hi, done):
                pool.tensor_tensor(dst, full, hi.bitcast(F32), ALU.subtract).then_inc(done, 1)

            def rest_w1_w2():
                pool.wait_ge(w_hi["w1"], 1)
                rest(W1[1][:], raws["w1"][:], W1[0][:], w_lo["w1"])
                pool.wait_ge(w_hi["w2"], 1)
                rest(W2[1][:], raws["w2"][:], W2[0][:], w_lo["w2"])

            def step(t, q, k):
                if live(t - 2):
                    g, slot = t - 2, (k - 2) % RING
                    pool.wait_ge(h1_hi, g + 1)
                    rest(h1T[1][:], h1T_full[:], h1T[0][:], h1_lo)
                if live(t - 3):
                    g, slot = t - 3, (k - 3) % RING
                    pool.wait_ge(mean_var_ok[1], g + 1)
                    pool.tensor_tensor(var_eps[1][:], mean_var[1][:, :, 1], eps2[:], ALU.add).then_inc(var_ok[1], 1)
                    pool.tensor_tensor(neg_mean[1][:], zero2[:], mean_var[1][:, :, 0], ALU.subtract)
                    pool.wait_ge(var_ok[1], g + 1)
                    if live(g - 1):
                        pool.wait_ge(x2_ok, g)
                    pool.tensor_tensor(rstd[1][:], var_eps[1][:], minus_half2[:], ALU.pow).then_inc(rstd_ok[1], 1)
                    pool.wait_ge(rstd_ok[1], g + 1)
                    pool.tensor_tensor(shift[1][:], neg_mean[1][:], rstd[1][:], ALU.mult).then_inc(shift_ok[1], 1)
                if live(t - 1):
                    g, slot = t - 1, (k - 1) % RING
                    pool.wait_ge(adj_hi, g + 1)
                    rest(adjT[slot][1][:], adjT_full[slot % 2][:], adjT[slot][0][:], adj_lo)
                    pool.wait_ge(mean_var_ok[0], g + 1)
                    pool.tensor_tensor(var_eps[0][:], mean_var[0][:, :, 1], eps2[:], ALU.add).then_inc(var_ok[0], 1)
                    pool.tensor_tensor(neg_mean[0][:], zero2[:], mean_var[0][:, :, 0], ALU.subtract)
                    pool.wait_ge(var_ok[0], g + 1)
                    if live(g - 1):
                        pool.wait_ge(x1_ok, g)
                    pool.tensor_tensor(rstd[0][:], var_eps[0][:], minus_half2[:], ALU.pow).then_inc(rstd_ok[0], 1)
                    pool.wait_ge(rstd_ok[0], g + 1)
                    pool.tensor_tensor(shift[0][:], neg_mean[0][:], rstd[0][:], ALU.mult).then_inc(shift_ok[0], 1)
                    pool.wait_ge(links_ok, g + 1)
                    pool.tensor_tensor(dinv[slot][:], links[slot][:], minus_half2[:], ALU.pow).then_inc(dinv_ok, 1)
                if live(t):
                    g, slot = t, k
                    if isinstance(g, int) and g == 1:
                        rest_w1_w2()
                    pool.wait_ge(x0_hi, g + 1)
                    rest(x0[1][:], x_in[slot][:], x0[0][:], x0_lo)
                if live(t - 2):
                    g, slot = t - 2, (k - 2) % RING
                    pool.wait_ge(h2_hi, g + 1)
                    rest(h2T[1][:], h2T_full[:], h2T[0][:], h2_lo)
                if live(t - 1):
                    g, slot = t - 1, (k - 1) % RING
                    pool.wait_ge(x1_ok, g + 1)
                    if live(g - 2):
                        pool.wait_ge(res_ok[1], g - 1)
                    if first(g):
                        pool.wait_ge(biases_loaded, 16 * N_BIASES)
                    pool.tensor_tensor(x1_b3[slot % 2][:], x1[:], b3_rows[:], ALU.add).then_inc(x1_b3_ok, 1)
                if live(t):
                    g, slot = t, k
                    pool.wait_ge(e_hi, g + 1)
                    if live(g - 1):
                        pool.wait_ge(ExT_mm, g)
                    rest(eT[1][:], eT_full[:], eT[0][:], e_lo)
                if live(t - 3):
                    g, slot = t - 3, (k - 3) % RING
                    pool.wait_ge(agg_tanh, g + 1)
                    if live(g - 1):
                        pool.wait_ge(x3_ok, g)
                    pool.tensor_tensor(res[2][:], agg[:], x2[slot % 2][:], ALU.add).then_inc(res_ok[2], 1)
                if live(t - 4):
                    g, slot = t - 4, (k - 4) % RING
                    pool.wait_ge(mean_var_ok[3], g + 1)
                    pool.tensor_tensor(var_eps[3][:], mean_var[3][:, :, 1], eps2[:], ALU.add).then_inc(var_ok[3], 1)
                    pool.tensor_tensor(neg_mean[3][:], zero2[:], mean_var[3][:, :, 0], ALU.subtract)
                    pool.wait_ge(var_ok[3], g + 1)
                    pool.tensor_tensor(rstd[3][:], var_eps[3][:], minus_half2[:], ALU.pow).then_inc(rstd_ok[3], 1)
                    pool.wait_ge(rstd_ok[3], g + 1)
                    pool.tensor_tensor(shift[3][:], neg_mean[3][:], rstd[3][:], ALU.mult).then_inc(shift_ok[3], 1)
                if live(t - 3):
                    g, slot = t - 3, (k - 3) % RING
                    pool.wait_ge(mean_var_ok[2], g + 1)
                    pool.tensor_tensor(var_eps[2][:], mean_var[2][:, :, 1], eps2[:], ALU.add).then_inc(var_ok[2], 1)
                    pool.tensor_tensor(neg_mean[2][:], zero2[:], mean_var[2][:, :, 0], ALU.subtract)
                    pool.wait_ge(var_ok[2], g + 1)
                    if live(g - 1):
                        pool.wait_ge(x3_ok, g)
                    pool.tensor_tensor(rstd[2][:], var_eps[2][:], minus_half2[:], ALU.pow).then_inc(rstd_ok[2], 1)
                    pool.wait_ge(rstd_ok[2], g + 1)
                    pool.tensor_tensor(shift[2][:], neg_mean[2][:], rstd[2][:], ALU.mult).then_inc(shift_ok[2], 1)

            pool.memset(eye[:], 0.0).then_inc(eye_cleared, 1)
            pool.wait_ge(eye_cleared, 1)
            pool.affine_select(out=eye[:], in_=eye[:], compare_op=ALU.not_equal, fill=1.0, base=0,
                               pattern=[[P, NT], [-1, N]], channel_multiplier=1).then_inc(consts_ready, 1)
            pool.wait_ge(consts_ready, N_CONSTS)
            pool.wait_ge(w_hi["w0"], 1)
            rest(W0[1][:], raws["w0"][:], W0[0][:], w_lo["w0"])
            steps(pool, step)


_INS = ['x', 'adj', 'L0_gnn_w', 'L0_gnn_a', 'L1_gnn_W1', 'L1_gnn_b1', 'L1_gnn_W2', 'L1_gnn_b2', 'L1_gnn_W3',
        'L1_gnn_b3', 'L2_gnn_W', 'L2_gnn_b', 'L3_gnn_W']


def kernel(**inputs):
    import numpy as _np
    import concourse.bacc as _bacc
    from concourse import mybir as _mybir
    from concourse.bass_utils import run_bass_kernel_spmd as _run

    nc = _bacc.Bacc("TRN2", target_bir_lowering=False, num_devices=1)
    arrays, args = {}, []
    for name in _INS:
        a = _np.ascontiguousarray(inputs[name])
        arrays[f"in_{name}_dram"] = a
        args.append(nc.dram_tensor(f"in_{name}_dram", a.shape, _mybir.dt.from_np(a.dtype), kind="ExternalInput").ap())
    args.append(nc.dram_tensor("out_0_dram", inputs['x'].shape, _mybir.dt.float32, kind="ExternalOutput").ap())
    resnorm_gnn_stack(nc, *args)
    r = _run(nc, [arrays], core_ids=[0])
    return r.results[0]["out_0_dram"]
```
